# Optimizing a Trainium2 kernel written in Bass

```python
import numpy as np
import jax
import jax.numpy as jnp

def _softmax(x, axis=-1):
    return jax.nn.softmax(x, axis=axis)

def _gelu(x):
    return jax.nn.gelu(x, approximate=True)

def _silu(x):
    return jax.nn.silu(x)

def _sigmoid(x):
    return jax.nn.sigmoid(x)

def _layernorm(x, axis=-1, eps=1e-05):
    m = jnp.mean(x, axis=axis, keepdims=True)
    v = jnp.var(x, axis=axis, keepdims=True)
    return (x - m) / jnp.sqrt(v + eps)

def _scatter_add(tgt, idx, src, axis=0):
    return tgt.at[idx].add(src)

def _segment_sum(src, seg, n):
    return jax.ops.segment_sum(src, seg, n)
kernel_name = 'mk_gnn_ffn_d2_gnn_r8_52bdd5'

def setup_inputs(seed: int=0):
    np.random.seed(seed)
    _w = jnp.asarray

    def _rec_inputs():
        import jax
        import jax.numpy as jnp
        _gk = jax.random.key(seed)
        x = -0.0003713 + 1 * jax.random.normal(jax.random.fold_in(_gk, 1), (6250, 256), jnp.float32)
        src = jax.random.randint(jax.random.fold_in(_gk, 2), (200000,), 0, 6250, jnp.int32)
        dst = jnp.minimum((6250 * jax.random.uniform(jax.random.fold_in(_gk, 3), (200000,)) ** 2.0).astype(jnp.int32), 49999)
        _o = jnp.argsort(dst, stable=True)
        src = src[_o]
        dst = dst[_o]
        edge_type_8 = jax.random.randint(jax.random.fold_in(_gk, 13), (200000,), 0, 8, jnp.int32)
        return (x, src, dst, edge_type_8)
    x, src, dst, edge_type_8 = _rec_inputs()

    def _L0_gnn_setup():
        import jax, jax.numpy as jnp
        import numpy as np
        N_NODES = 6250
        N_EDGES = 100000
        IN_FEAT = 256
        OUT_FEAT = 256
        NUM_RELS = 8
        ALPHA = 0.5
        key = jax.random.key(seed)
        k1, k2, k3, k4, k5, k6 = jax.random.split(key, 6)
        x = jax.random.normal(k1, (N_NODES, IN_FEAT), dtype=jnp.float32)
        edge_index = jax.random.randint(k2, (2, N_EDGES), 0, N_NODES, dtype=jnp.int64)
        edge_type = jax.random.randint(k3, (N_EDGES,), 0, NUM_RELS, dtype=jnp.int64)
        gain = float(np.sqrt(2.0))
        lim_w = gain * float(np.sqrt(6.0 / (IN_FEAT + OUT_FEAT)))
        weight = jax.random.uniform(k4, (NUM_RELS, IN_FEAT, OUT_FEAT), dtype=jnp.float32, minval=-lim_w, maxval=lim_w)
        loop_weight = jax.random.uniform(k5, (IN_FEAT, OUT_FEAT), dtype=jnp.float32, minval=-lim_w, maxval=lim_w)
        h_bias = jnp.zeros((OUT_FEAT,), dtype=jnp.float32)
        return {'edge_index': edge_index, 'x': x, 'edge_type': edge_type, 'weight': weight, 'h_bias': h_bias, 'loop_weight': loop_weight}
    _L0_gnn_all = _L0_gnn_setup()
    _L0_gnn_in = {k: v for k, v in _L0_gnn_all.items() if k in ('weight', 'h_bias', 'loop_weight')}
    del _L0_gnn_all

    def _L0_ffn_setup():
        import jax, jax.numpy as jnp
        import numpy as np
        B, N, D = (16, 512, 256)
        NUM_EXPERTS, TOP_K, HEADS = (4, 2, 4)
        N_EDGES = 131072
        LN_EPS = 1e-05

        def _layernorm(x, g, b):
            mu = x.mean(-1, keepdims=True)
            var = ((x - mu) ** 2).mean(-1, keepdims=True)
            return (x - mu) * jax.lax.rsqrt(var + LN_EPS) * g + b

        def _forward(x, edge_index, W_gat, att_src, att_dst, b_gat, ln_gamma, ln_beta, W1, b1, W2, b2):
            Bc, Nc, Dc = x.shape
            M = Bc * Nc
            x_flat = x.reshape(M, Dc)
            h = (x_flat @ W_gat).reshape(M, HEADS, NUM_EXPERTS)
            loops = jnp.arange(M, dtype=edge_index.dtype)
            src = jnp.concatenate([edge_index[0], loops])
            dst = jnp.concatenate([edge_index[1], loops])
            a_src = (h * att_src).sum(-1)
            a_dst = (h * att_dst).sum(-1)
            e = jax.nn.leaky_relu(a_src[src] + a_dst[dst], negative_slope=0.2)
            e_max = jax.ops.segment_max(e, dst, num_segments=M)
            ee = jnp.exp(e - e_max[dst])
            denom = jax.ops.segment_sum(ee, dst, num_segments=M)
            alpha = ee / (denom[dst] + 1e-16)
            msg = h[src] * alpha[:, :, None]
            agg = jax.ops.segment_sum(msg, dst, num_segments=M).reshape(M, HEADS * NUM_EXPERTS) + b_gat
            scores = _layernorm(agg, ln_gamma, ln_beta).reshape(M, HEADS, NUM_EXPERTS).mean(1)
            scores = scores.reshape(Bc, Nc, NUM_EXPERTS)
            topk_s, topk_i = jax.lax.top_k(scores, TOP_K)
            w = jax.nn.softmax(topk_s, axis=-1)
            out = jnp.zeros_like(x)
            for ei in range(NUM_EXPERTS):
                g = jnp.where(topk_i == ei, w, 0.0).sum(-1)
                hh = jax.nn.gelu(x @ W1[ei] + b1[ei], approximate=False)
                out = out + g[..., None] * (hh @ W2[ei] + b2[ei])
            return out
        key = jax.random.key(seed)
        ks = jax.random.split(key, 8)
        s = 0.05
        return {'x': jax.random.normal(ks[0], (B, N, D), jnp.float32), 'W_gat': jax.random.normal(ks[1], (D, HEADS * NUM_EXPERTS), jnp.float32) * s, 'att_src': jax.random.normal(ks[2], (HEADS, NUM_EXPERTS), jnp.float32) * s, 'att_dst': jax.random.normal(ks[3], (HEADS, NUM_EXPERTS), jnp.float32) * s, 'b_gat': jnp.zeros((HEADS * NUM_EXPERTS,), jnp.float32), 'ln_gamma': jnp.ones((HEADS * NUM_EXPERTS,), jnp.float32), 'ln_beta': jnp.zeros((HEADS * NUM_EXPERTS,), jnp.float32), 'W1': jax.random.normal(ks[4], (NUM_EXPERTS, D, 2 * D), jnp.float32) * s, 'b1': jnp.zeros((NUM_EXPERTS, 2 * D), jnp.float32), 'W2': jax.random.normal(ks[5], (NUM_EXPERTS, 2 * D, D), jnp.float32) * s, 'b2': jnp.zeros((NUM_EXPERTS, D), jnp.float32), 'edge_index': jax.random.randint(ks[6], (2, N_EDGES), 0, B * N, jnp.int32)}
    _L0_ffn_all = _L0_ffn_setup()
    _L0_ffn_in = {k: v for k, v in _L0_ffn_all.items() if k in ('W_gat', 'att_src', 'att_dst', 'b_gat', 'ln_gamma', 'ln_beta', 'W1', 'b1', 'W2', 'b2', 'edge_index')}
    del _L0_ffn_all

    def _L1_gnn_setup():
        import jax, jax.numpy as jnp
        import numpy as np
        N = 12500
        E = 200000
        IN_FEATS = 256
        OUT_FEATS = 256
        MAXK = 32

        def _maxk(x, k):
            _, idx = jax.lax.top_k(x, k)
            rows = jnp.arange(x.shape[0])[:, None]
            mask = jnp.zeros_like(x).at[rows, idx].set(1.0)
            return x * mask
        key = jax.random.key(seed)
        k1, k2, k3, k4, k5 = jax.random.split(key, 5)
        feat = jax.random.normal(k1, (N, IN_FEATS), dtype=jnp.float32)
        W_self = jax.random.normal(k2, (IN_FEATS, OUT_FEATS), dtype=jnp.float32) * (1.0 / np.sqrt(IN_FEATS))
        W_neigh = jax.random.normal(k3, (IN_FEATS, OUT_FEATS), dtype=jnp.float32) * (1.0 / np.sqrt(IN_FEATS))
        src = jax.random.randint(k4, (E,), 0, N, dtype=jnp.int64)
        dst = jax.random.randint(k5, (E,), 0, N, dtype=jnp.int64)
        return {'feat': feat, 'W_self': W_self, 'W_neigh': W_neigh, 'src': src, 'dst': dst}
    _L1_gnn_all = _L1_gnn_setup()
    _L1_gnn_in = {k: v for k, v in _L1_gnn_all.items() if k in ('W_self', 'W_neigh')}
    del _L1_gnn_all

    def _L1_ffn_setup():
        import jax, jax.numpy as jnp
        import numpy as np
        DIM = 256
        H = 8
        D = 64
        G = 64
        INNER = H * D
        SCALE = D ** (-0.5)
        key = jax.random.key(seed)
        ks = jax.random.split(key, 12)
        B, N = (4, 2048)
        x = jax.random.normal(ks[0], (B, N, DIM), dtype=jnp.float32)
        s = lambda fan_in: 1.0 / np.sqrt(fan_in)
        W_fx = jax.random.normal(ks[1], (DIM, INNER), dtype=jnp.float32) * s(DIM)
        b_fx = jnp.zeros((INNER,), dtype=jnp.float32)
        W_x = jax.random.normal(ks[2], (DIM, INNER), dtype=jnp.float32) * s(DIM)
        b_x = jnp.zeros((INNER,), dtype=jnp.float32)
        A = jax.random.normal(ks[3], (G, D), dtype=jnp.float32)
        Q, _ = jnp.linalg.qr(A.T)
        W_slice = Q[:, :G].astype(jnp.float32)
        b_slice = jnp.zeros((G,), dtype=jnp.float32)
        W_q = jax.random.normal(ks[4], (D, D), dtype=jnp.float32) * s(D)
        W_k = jax.random.normal(ks[5], (D, D), dtype=jnp.float32) * s(D)
        W_v = jax.random.normal(ks[6], (D, D), dtype=jnp.float32) * s(D)
        W_out = jax.random.normal(ks[7], (INNER, DIM), dtype=jnp.float32) * s(INNER)
        b_out = jnp.zeros((DIM,), dtype=jnp.float32)
        temperature = jnp.ones((1, H, 1, 1), dtype=jnp.float32) * 0.5
        return {'x': x, 'W_fx': W_fx, 'b_fx': b_fx, 'W_x': W_x, 'b_x': b_x, 'W_slice': W_slice, 'b_slice': b_slice, 'W_q': W_q, 'W_k': W_k, 'W_v': W_v, 'W_out': W_out, 'b_out': b_out, 'temperature': temperature}
    _L1_ffn_all = _L1_ffn_setup()
    _L1_ffn_in = {k: v for k, v in _L1_ffn_all.items() if k in ('W_fx', 'b_fx', 'W_x', 'b_x', 'W_slice', 'b_slice', 'W_q', 'W_k', 'W_v', 'W_out', 'b_out', 'temperature')}
    del _L1_ffn_all
    return {'x': x, 'src': src, 'dst': dst, 'edge_type_8': edge_type_8, 'L0_gnn_weight': _L0_gnn_in['weight'], 'L0_gnn_h_bias': _L0_gnn_in['h_bias'], 'L0_gnn_loop_weight': _L0_gnn_in['loop_weight'], 'L0_ffn_W_gat': _L0_ffn_in['W_gat'], 'L0_ffn_att_src': _L0_ffn_in['att_src'], 'L0_ffn_att_dst': _L0_ffn_in['att_dst'], 'L0_ffn_b_gat': _L0_ffn_in['b_gat'], 'L0_ffn_ln_gamma': _L0_ffn_in['ln_gamma'], 'L0_ffn_ln_beta': _L0_ffn_in['ln_beta'], 'L0_ffn_W1': _L0_ffn_in['W1'], 'L0_ffn_b1': _L0_ffn_in['b1'], 'L0_ffn_W2': _L0_ffn_in['W2'], 'L0_ffn_b2': _L0_ffn_in['b2'], 'L0_ffn_edge_index': _L0_ffn_in['edge_index'], 'L1_gnn_W_self': _L1_gnn_in['W_self'], 'L1_gnn_W_neigh': _L1_gnn_in['W_neigh'], 'L1_ffn_W_fx': _L1_ffn_in['W_fx'], 'L1_ffn_b_fx': _L1_ffn_in['b_fx'], 'L1_ffn_W_x': _L1_ffn_in['W_x'], 'L1_ffn_b_x': _L1_ffn_in['b_x'], 'L1_ffn_W_slice': _L1_ffn_in['W_slice'], 'L1_ffn_b_slice': _L1_ffn_in['b_slice'], 'L1_ffn_W_q': _L1_ffn_in['W_q'], 'L1_ffn_W_k': _L1_ffn_in['W_k'], 'L1_ffn_W_v': _L1_ffn_in['W_v'], 'L1_ffn_W_out': _L1_ffn_in['W_out'], 'L1_ffn_b_out': _L1_ffn_in['b_out'], 'L1_ffn_temperature': _L1_ffn_in['temperature']}

def reference(x, src, dst, edge_type_8, L0_gnn_weight, L0_gnn_h_bias, L0_gnn_loop_weight, L0_ffn_W_gat, L0_ffn_att_src, L0_ffn_att_dst, L0_ffn_b_gat, L0_ffn_ln_gamma, L0_ffn_ln_beta, L0_ffn_W1, L0_ffn_b1, L0_ffn_W2, L0_ffn_b2, L0_ffn_edge_index, L1_gnn_W_self, L1_gnn_W_neigh, L1_ffn_W_fx, L1_ffn_b_fx, L1_ffn_W_x, L1_ffn_b_x, L1_ffn_W_slice, L1_ffn_b_slice, L1_ffn_W_q, L1_ffn_W_k, L1_ffn_W_v, L1_ffn_W_out, L1_ffn_b_out, L1_ffn_temperature):
    import jax
    import jax.numpy as jnp

    def _L0_gnn_ref(edge_index, x, edge_type, weight, h_bias, loop_weight):
        import jax, jax.numpy as jnp
        import numpy as np
        N_NODES = 6250
        N_EDGES = 100000
        IN_FEAT = 256
        OUT_FEAT = 256
        NUM_RELS = 8
        ALPHA = 0.5
        num_nodes = x.shape[0]
        src, dst = (edge_index[0], edge_index[1])
        hx = jnp.einsum('ni,rio->rno', x, weight)
        msg = hx[edge_type, src]
        agg = jax.ops.segment_sum(msg, dst, num_segments=num_nodes)
        node_repr = agg * jnp.asarray(ALPHA, x.dtype) ** 0.5
        node_repr = node_repr + h_bias
        loop_message = x @ loop_weight
        node_repr = node_repr + loop_message * jnp.asarray(1.0 - ALPHA, x.dtype) ** 0.5
        return node_repr

    def _L0_ffn_ref(x, W_gat, att_src, att_dst, b_gat, ln_gamma, ln_beta, W1, b1, W2, b2, edge_index):
        import jax, jax.numpy as jnp
        import numpy as np
        B, N, D = (16, 512, 256)
        NUM_EXPERTS, TOP_K, HEADS = (4, 2, 4)
        N_EDGES = 131072
        LN_EPS = 1e-05

        def _layernorm(x, g, b):
            mu = x.mean(-1, keepdims=True)
            var = ((x - mu) ** 2).mean(-1, keepdims=True)
            return (x - mu) * jax.lax.rsqrt(var + LN_EPS) * g + b

        def _forward(x, edge_index, W_gat, att_src, att_dst, b_gat, ln_gamma, ln_beta, W1, b1, W2, b2):
            Bc, Nc, Dc = x.shape
            M = Bc * Nc
            x_flat = x.reshape(M, Dc)
            h = (x_flat @ W_gat).reshape(M, HEADS, NUM_EXPERTS)
            loops = jnp.arange(M, dtype=edge_index.dtype)
            src = jnp.concatenate([edge_index[0], loops])
            dst = jnp.concatenate([edge_index[1], loops])
            a_src = (h * att_src).sum(-1)
            a_dst = (h * att_dst).sum(-1)
            e = jax.nn.leaky_relu(a_src[src] + a_dst[dst], negative_slope=0.2)
            e_max = jax.ops.segment_max(e, dst, num_segments=M)
            ee = jnp.exp(e - e_max[dst])
            denom = jax.ops.segment_sum(ee, dst, num_segments=M)
            alpha = ee / (denom[dst] + 1e-16)
            msg = h[src] * alpha[:, :, None]
            agg = jax.ops.segment_sum(msg, dst, num_segments=M).reshape(M, HEADS * NUM_EXPERTS) + b_gat
            scores = _layernorm(agg, ln_gamma, ln_beta).reshape(M, HEADS, NUM_EXPERTS).mean(1)
            scores = scores.reshape(Bc, Nc, NUM_EXPERTS)
            topk_s, topk_i = jax.lax.top_k(scores, TOP_K)
            w = jax.nn.softmax(topk_s, axis=-1)
            out = jnp.zeros_like(x)
            for ei in range(NUM_EXPERTS):
                g = jnp.where(topk_i == ei, w, 0.0).sum(-1)
                hh = jax.nn.gelu(x @ W1[ei] + b1[ei], approximate=False)
                out = out + g[..., None] * (hh @ W2[ei] + b2[ei])
            return out
        return _forward(x, edge_index, W_gat, att_src, att_dst, b_gat, ln_gamma, ln_beta, W1, b1, W2, b2)

    def _L1_gnn_ref(feat, W_self, W_neigh, src, dst):
        import jax, jax.numpy as jnp
        import numpy as np
        N = 12500
        E = 200000
        IN_FEATS = 256
        OUT_FEATS = 256
        MAXK = 32

        def _maxk(x, k):
            _, idx = jax.lax.top_k(x, k)
            rows = jnp.arange(x.shape[0])[:, None]
            mask = jnp.zeros_like(x).at[rows, idx].set(1.0)
            return x * mask
        n = feat.shape[0]
        h_self = feat @ W_self
        h_neigh = feat @ W_neigh
        h_sparse = _maxk(h_neigh, MAXK)
        msg = h_sparse[src]
        summed = jax.ops.segment_sum(msg, dst, num_segments=n)
        deg = jax.ops.segment_sum(jnp.ones((src.shape[0],), dtype=feat.dtype), dst, num_segments=n)
        neigh = summed / jnp.maximum(deg, 1.0)[:, None]
        return h_self + neigh

    def _L1_ffn_ref(x, W_fx, b_fx, W_x, b_x, W_slice, b_slice, W_q, W_k, W_v, W_out, b_out, temperature):
        import jax, jax.numpy as jnp
        import numpy as np
        DIM = 256
        H = 8
        D = 64
        G = 64
        INNER = H * D
        SCALE = D ** (-0.5)
        B, N, _ = x.shape
        fx_mid = (x @ W_fx + b_fx).reshape(B, N, H, D).transpose(0, 2, 1, 3)
        x_mid = (x @ W_x + b_x).reshape(B, N, H, D).transpose(0, 2, 1, 3)
        temp = jnp.clip(temperature, 0.1, 5.0)
        slice_weights = jax.nn.softmax((x_mid @ W_slice + b_slice) / temp, axis=-1)
        slice_norm = slice_weights.sum(axis=2)
        slice_token = jnp.einsum('bhnc,bhng->bhgc', fx_mid, slice_weights)
        slice_token = slice_token / (slice_norm[..., None] + 1e-05)
        q = slice_token @ W_q
        k = slice_token @ W_k
        v = slice_token @ W_v
        attn = jax.nn.softmax(jnp.einsum('bhgc,bhkc->bhgk', q, k) * SCALE, axis=-1)
        out_slice = jnp.einsum('bhgk,bhkc->bhgc', attn, v)
        out_x = jnp.einsum('bhgc,bhng->bhnc', out_slice, slice_weights)
        out_x = out_x.transpose(0, 2, 1, 3).reshape(B, N, INNER)
        return out_x @ W_out + b_out
    edge_index = jnp.stack([src, dst])
    x = x + _L0_gnn_ref(edge_index, _layernorm(x, axis=-1), edge_type_8, L0_gnn_weight, L0_gnn_h_bias, L0_gnn_loop_weight)
    x = x + _L0_ffn_ref(_layernorm(x, axis=-1)[None], L0_ffn_W_gat, L0_ffn_att_src, L0_ffn_att_dst, L0_ffn_b_gat, L0_ffn_ln_gamma, L0_ffn_ln_beta, L0_ffn_W1, L0_ffn_b1, L0_ffn_W2, L0_ffn_b2, L0_ffn_edge_index)[0]
    x = x + _L1_gnn_ref(_layernorm(x, axis=-1), L1_gnn_W_self, L1_gnn_W_neigh, src, dst)
    x = x + _L1_ffn_ref(_layernorm(x, axis=-1)[None], L1_ffn_W_fx, L1_ffn_b_fx, L1_ffn_W_x, L1_ffn_b_x, L1_ffn_W_slice, L1_ffn_b_slice, L1_ffn_W_q, L1_ffn_W_k, L1_ffn_W_v, L1_ffn_W_out, L1_ffn_b_out, L1_ffn_temperature)[0]
    return x

_drawn_inputs = setup_inputs


def setup_inputs(seed=0):
    import zlib

    import numpy as np

    out = dict(_drawn_inputs(seed))
    spreads = {'L0_gnn_h_bias': (0.0, 0.283),
     'L0_ffn_b_gat': (0.0, 0.1),
     'L0_ffn_ln_gamma': (1.0, 0.6),
     'L0_ffn_ln_beta': (0.0, 0.509),
     'L0_ffn_b1': (0.0, 0.8),
     'L0_ffn_b2': (0.0, 0.639),
     'L1_ffn_b_fx': (0.0, 0.478),
     'L1_ffn_b_x': (0.0, 0.8),
     'L1_ffn_b_slice': (0.0, 0.8),
     'L1_ffn_b_out': (0.0, 1.502),
     'L1_ffn_temperature': (0.5, 0.6)}
    factors = {'L0_ffn_att_src': 5.417,
     'L0_ffn_att_dst': 8.0,
     'L1_gnn_W_neigh': 2.778,
     'L1_ffn_W_fx': 7.264,
     'L1_ffn_W_x': 8.0,
     'L1_ffn_W_slice': 8.0,
     'L1_ffn_W_q': 8.0,
     'L1_ffn_W_k': 8.0,
     'L1_ffn_W_v': 3.214,
     'L1_ffn_W_out': 2.993}
    for name, (base, spread) in spreads.items():
        noise = np.random.default_rng([zlib.crc32(name.encode()), seed]).standard_normal(out[name].shape)
        drawn = base * np.exp(spread * noise) if base else spread * noise
        out[name] = jnp.asarray(drawn.astype(out[name].dtype))
    for name, factor in factors.items():
        out[name] = (out[name] * factor).astype(out[name].dtype)
    return out
```

```python
from contextlib import ExitStack

import concourse.bass as bass
from concourse import mybir

F32 = mybir.dt.float32
I32 = mybir.dt.int32
ALU = mybir.AluOpType
ACT = mybir.ActivationFunctionType
AX_X = mybir.AxisListType.X
RMAX = bass.bass_isa.ReduceOp.max

P = 128
D = 256
KH = D // P
N = 6250
NW = -(-N // P)
NP = NW * P
LAST = N - (NW - 1) * P
RELS = 8
E = 200000
GROUP = 4
BODY = 16
NT = -(-E // (P * BODY)) * BODY
NG = NT // GROUP
RANGED = 7
GROWS = 98
GE = 131072
GNT = GE // P
GBODY = 16
HEADS, EXPERTS = 4, 4
HE = HEADS * EXPERTS
SRCW = HE + HEADS
DSTW = 2 * HEADS
FF = 512
NB = FF // P
ACCW = D + 1
BANK = 512
NOWHERE = 8191
EPS = 1e-5
SPREAD = 16.0
LOWEST = -3.0e38
SH, SD, SG = 8, 64, 64
INNER = SH * SD


def each_window(eng, body):
    body(0, 0)
    body(1, 1)
    with eng.Fori(1, NW // 2) as i:
        body(2 * i, 0)
        body(2 * i + 1, 1)
    body(NW - 1, 0)


def wait_if(eng, sem, value):
    if not isinstance(value, int) or value > 0:
        eng.wait_ge(sem, value)


class Named:
    pass


class Phase(ExitStack):

    def __init__(self, nc):
        super().__init__()
        self.nc, self.sems = nc, []

    def semaphore(self, name):
        self.sems.append(self.nc.alloc_semaphore(name))
        return self.sems[-1]

    def __exit__(self, *raised):
        out = super().__exit__(*raised)
        if raised[0] is None:
            self.nc.clear_and_free_semaphores(self.sems)
            self.nc.all_engine_barrier()
        return out


def stand(eng, sem, value, passed):
    if not isinstance(value, int) or value > 0:
        eng.wait_ge(sem, value)
        eng.sem_inc(passed, 1)


class Chain:

    def __init__(self, eng, sem):
        self.eng, self.sem, self.n = eng, sem, 0

    def did(self, instruction):
        instruction.then_inc(self.sem, 1)
        self.n += 1

    def settled(self):
        self.eng.wait_ge(self.sem, self.n)



def constants(nc, b, m):
    with Phase(nc) as ctx:
        sem = lambda name: ctx.semaphore(name)
        sb = lambda name, shape, dt: ctx.enter_context(nc.sbuf_tensor(name, shape, dt))
        loaded = sem("c_loaded")
        filled = sem("c_filled")
        ranged = sem("c_ranged")
        stored = sem("c_stored")
        spread = sem("c_spread")
        prepared = sem("c_prepared")
        etype = sb("c_type", [P, NT], I32)
        rows = sb("c_rows", [GROWS, NG // GROWS, GROUP * P], I32)
        inside = sb("c_inside", [GROWS, NG // GROWS, GROUP * P], F32)
        lowest = sb("c_lowest", [GROWS, NG // GROWS], I32)
        highest = sb("c_highest", [GROWS, NG // GROWS], I32)
        wlow = sb("c_wlow", [GROWS, NG // GROWS], I32)
        whigh = sb("c_whigh", [GROWS, NG // GROWS], I32)
        wbase = sb("c_wbase", [GROWS, NG // GROWS], I32)
        wspan = sb("c_wspan", [GROWS, NG // GROWS], I32)
        basis = sb("c_basis", [P, NG], I32)
        spans = sb("c_spans", [1, NG], I32)
        block = ctx.enter_context(nc.Block())

        @block.sync
        def _(eng):
            eng.dma_start(rows[:, :, :], m["dst_rows"]).then_inc(loaded, 16)
            eng.dma_start(b.esrc[:, :], m["src_cols"]).then_inc(loaded, 16)
            eng.dma_start(b.edsti[:, :], m["dst_cols"]).then_inc(loaded, 16)
            eng.dma_start(etype[:, :], m["type_cols"]).then_inc(loaded, 16)
            eng.dma_start(b.x[:, :, :], m["x"].rearrange("(w p) d -> p w d", p=P)).then_inc(loaded, 16)
            eng.wait_ge(ranged, RANGED)
            eng.dma_start(m["scr_base"].rearrange("(r g) -> r g", r=GROWS), wbase[:, :]).then_inc(stored, 16)
            eng.dma_start(m["scr_span"].rearrange("(r g) -> r g", r=GROWS), wspan[:, :]).then_inc(stored, 16)
            eng.wait_ge(stored, 32)
            eng.dma_start(b.wbase[:, :], m["scr_base"].rearrange("(a g) -> a g", a=1)).then_inc(spread, 16)
            eng.dma_start(spans[:, :], m["scr_span"].rearrange("(a g) -> a g", a=1)).then_inc(spread, 16)
            eng.dma_start(basis[:, :], m["scr_base"].rearrange("(a g) -> a g", a=1).broadcast_to([P, NG])).then_inc(spread, 16)
            eng.wait_ge(spread, 48)
            eng.wait_ge(loaded, 80)

        @block.gpsimd
        def _(eng):
            g = Chain(eng, filled)
            g.did(eng.memset(b.ident[:, :], 0.0))
            g.did(eng.memset(b.ones[:, :], 1.0))
            g.did(eng.iota(b.ramp[:, :], pattern=[[1, 2 * P]], base=0, channel_multiplier=0,
                           allow_small_or_imprecise_dtypes=True))
            g.did(eng.iota(b.wstart[:, :], pattern=[[P, NW]], base=0, channel_multiplier=0,
                           allow_small_or_imprecise_dtypes=True))
            g.settled()
            g.did(eng.affine_select(out=b.ident[:, :], in_=b.ident[:, :], compare_op=ALU.not_equal,
                                    fill=1.0, base=0, pattern=[[-1, P]], channel_multiplier=1))
            g.settled()

        @block.vector
        def _(eng):
            v = Chain(eng, ranged)
            eng.wait_ge(loaded, 80)
            v.did(eng.tensor_reduce(lowest[:, :], rows[:, :, :], AX_X, ALU.min))
            v.did(eng.scalar_tensor_tensor(inside[:, :, :], rows[:, :, :], float(N), rows[:, :, :],
                                           ALU.is_lt, ALU.mult))
            v.settled()
            v.did(eng.tensor_reduce(highest[:, :], inside[:, :, :], AX_X, ALU.max))
            v.settled()
            v.did(eng.tensor_scalar(wlow[:, :], lowest[:, :], 7, None, ALU.arith_shift_right))
            v.did(eng.tensor_scalar(whigh[:, :], highest[:, :], 7, None, ALU.arith_shift_right))
            v.settled()
            v.did(eng.tensor_scalar(wbase[:, :], wlow[:, :], float(NW - 2), None, ALU.min))
            v.settled()
            v.did(eng.tensor_tensor(wspan[:, :], whigh[:, :], wbase[:, :], ALU.subtract))
            assert v.n == RANGED
            p = Chain(eng, prepared)
            p.did(eng.scalar_tensor_tensor(b.erow[:, :], b.esrc[:, :], float(RELS), etype[:, :],
                                           ALU.mult, ALU.add))
            eng.wait_ge(spread, 48)
            p.did(eng.scalar_tensor_tensor(
                b.edst[:, :].rearrange("p (g t) -> p g t", t=GROUP),
                basis[:, :].unsqueeze(2).broadcast_to([P, NG, GROUP]), float(-P),
                b.edsti[:, :].rearrange("p (g t) -> p g t", t=GROUP), ALU.mult, ALU.add))
            p.did(eng.tensor_reduce(b.maxspan[:, :], spans[:, :], AX_X, ALU.max))
            p.settled()



def row_statistics(nc, b, use):
    with Phase(nc) as ctx:
        stats = ctx.enter_context(nc.sbuf_tensor(f"{use}_stats", [P, NW, 6], F32))
        work = ctx.enter_context(nc.sbuf_tensor(f"{use}_work", [P, 4, NW], F32))
        std = ctx.enter_context(nc.sbuf_tensor(f"{use}_std", [P, NW], F32))
        counted = ctx.semaphore(f"{use}_counted")
        combined = ctx.semaphore(f"{use}_combined")
        rooted = ctx.semaphore(f"{use}_rooted")
        block = ctx.enter_context(nc.Block())
        even = lambda n: stats[:, :, n]
        odd = lambda n: stats[:, :, 3 + n]
        STEPS = 7
        RUN = 7
        assert NW % RUN == 0

        @block.vector
        def _(eng):
            with eng.Fori(0, NW // RUN) as i:
                for q in range(RUN):
                    w = RUN * i + q
                    eng.bn_stats(stats[:, w, :], b.x[:, w, :]).then_inc(counted, 1)
            eng.wait_ge(counted, NW)
            v = Chain(eng, combined)
            v.did(eng.tensor_tensor(work[:, 0, :], even(1), odd(1), ALU.add))
            v.did(eng.tensor_tensor(work[:, 1, :], even(1), odd(1), ALU.subtract))
            v.did(eng.tensor_tensor(work[:, 2, :], even(2), odd(2), ALU.add))
            v.settled()
            v.did(eng.tensor_scalar(b.mean[:, :], work[:, 0, :], 0.5, None, ALU.mult))
            v.did(eng.scalar_tensor_tensor(work[:, 3, :], work[:, 1, :], 0.25, work[:, 1, :], ALU.mult, ALU.mult))
            v.did(eng.tensor_scalar(work[:, 2, :], work[:, 2, :], 1.0 / D, EPS, ALU.mult, ALU.add))
            v.settled()
            v.did(eng.tensor_tensor(b.rstd[:, :], work[:, 2, :], work[:, 3, :], ALU.add))
            assert v.n == STEPS
            eng.wait_ge(rooted, 1)
            v.did(eng.reciprocal(b.rstd[:, :], std[:, :]))
            v.settled()

        @block.scalar
        def _(eng):
            eng.wait_ge(combined, STEPS)
            eng.activation(std[:, :], b.rstd[:, :], ACT.Sqrt).then_inc(rooted, 1)



def relation_table(nc, b, m):
    PER = RELS * D // BANK
    with Phase(nc) as ctx:
        sem = lambda name: ctx.semaphore(name)
        sb = lambda name, shape: ctx.enter_context(nc.sbuf_tensor(name, shape, F32))
        pb = lambda name: ctx.enter_context(nc.psum_tensor(name, [P, BANK], F32))
        weights = sb("r_weights", [P, KH, RELS, D])
        loopw = sb("r_loopw", [P, KH, D])
        xn = [sb(f"r_xn{s}", [P, D]) for s in range(2)]
        xt = [sb(f"r_xt{s}", [P, KH, P]) for s in range(2)]
        stage = [sb(f"r_stage{s}", [P, RELS * D]) for s in range(2)]
        turned = [pb(f"r_turned{s}") for s in range(2)]
        product = [pb(f"r_product{c}") for c in range(PER)]
        looped = pb("r_looped")
        loaded = sem("r_loaded")
        normed = sem("r_normed")
        transposed = sem("r_transposed")
        copied = sem("r_copied")
        multiplied = sem("r_multiplied")
        evacuated = sem("r_evacuated")
        loopdone = sem("r_loopdone")
        stored = [sem(f"r_stored{s}") for s in range(2)]
        zeroed = sem("r_zeroed")
        block = ctx.enter_context(nc.Block())
        table = m["table1"].rearrange("(w p) c -> w p c", p=P)

        @block.sync
        def _(eng):
            for k in range(KH):
                eng.dma_start(weights[:, k, :, :], m["weight"][:, k * P:(k + 1) * P, :].rearrange("r p o -> p r o")).then_inc(loaded, 16)
            eng.dma_start(loopw[:, :, :], m["loop_weight"].rearrange("(k p) o -> p k o", p=P)).then_inc(loaded, 16)

            def body(w, s):
                eng.wait_ge(evacuated, (w + 1) * (PER + 1))
                eng.dma_start(table[w], stage[s][:, :]).then_inc(stored[s], 16)
            each_window(eng, body)
            eng.wait_ge(stored[0], 16 * (NW // 2 + 1))
            eng.wait_ge(stored[1], 16 * (NW // 2))

        @block.vector
        def _(eng):
            eng.memset(b.acc[:, :, D:ACCW], 0.0).then_inc(zeroed, 1)

            def body(w, s):
                wait_if(eng, transposed, w - 1)
                eng.tensor_scalar(xn[s][:, :], b.x[:, w, :], b.mean[:, bass.ds(w, 1)], b.rstd[:, bass.ds(w, 1)],
                                  ALU.subtract, ALU.mult).then_inc(normed, 1)
            each_window(eng, body)
            eng.wait_ge(zeroed, 1)

        @block.tensor
        def _(eng):
            def turn(w, s):
                eng.wait_ge(normed, w + 1)
                wait_if(eng, copied, w - 1)
                eng.transpose(turned[s][:, 0:P], xn[s][:, 0:P], b.ident[:, :])
                eng.transpose(turned[s][:, P:D], xn[s][:, P:D], b.ident[:, :]).then_inc(transposed, 1)

            def body(w, s):
                if not (isinstance(w, int) and w == NW - 1):
                    turn(w + 1, 1 - s)
                eng.wait_ge(copied, w + 1)
                for c in range(PER):
                    wait_if(eng, evacuated, w * (PER + 1) - PER + c)
                    for k in range(KH):
                        mm = eng.matmul(product[c][:, :], xt[s][:, k, :],
                                        weights[:, k, 2 * c:2 * c + 2, :].rearrange("p r o -> p (r o)"),
                                        start=(k == 0), stop=(k == KH - 1))
                    mm.then_inc(multiplied, 1)
                wait_if(eng, evacuated, w * (PER + 1))
                for k in range(KH):
                    mm = eng.matmul(looped[:, 0:D], xt[s][:, k, :], loopw[:, k, :],
                                    start=(k == 0), stop=(k == KH - 1))
                mm.then_inc(multiplied, 1)

            eng.wait_ge(loaded, 16 * (KH + 1))
            turn(0, 0)
            each_window(eng, body)

        @block.scalar
        def _(eng):
            def body(w, s):
                eng.wait_ge(transposed, w + 1)
                wait_if(eng, multiplied, (w - 1) * (PER + 1))
                eng.activation(xt[s][:, :, :].rearrange("p k n -> p (k n)"), turned[s][:, 0:D],
                               ACT.Copy).then_inc(copied, 1)

            def evacuate(w, s):
                if not isinstance(w, int) or w >= 2:
                    eng.wait_ge(stored[s], (w - s) * 8)
                for c in range(PER):
                    eng.wait_ge(multiplied, w * (PER + 1) + c + 1)
                    eng.activation(stage[s][:, c * BANK:(c + 1) * BANK], product[c][:, :],
                                   ACT.Copy).then_inc(evacuated, 1)
                eng.wait_ge(multiplied, (w + 1) * (PER + 1))
                eng.activation(b.acc[:, w, 0:D], looped[:, 0:D], ACT.Copy).then_inc(evacuated, 1)

            def both(w, s):
                if not (isinstance(w, int) and w == NW - 1):
                    body(w + 1, 1 - s)
                evacuate(w, s)

            body(0, 0)
            each_window(eng, both)



def edge_sums(nc, b, table, rows, use):
    HALF = BODY // 2
    ONEHOTS = 4
    with Phase(nc) as ctx:
        sem = lambda name: ctx.semaphore(name)
        ring = ctx.enter_context(nc.sbuf_tensor(f"{use}_ring", [P, BODY, ACCW], F32))
        index = [ctx.enter_context(nc.sbuf_tensor(f"{use}_index{h}", [P, HALF], I32)) for h in range(2)]
        onehot = [ctx.enter_context(nc.sbuf_tensor(f"{use}_onehot{s}", [P, 2 * P], F32)) for s in range(ONEHOTS)]
        sums = [ctx.enter_context(nc.psum_tensor(f"{use}_sums{s}", [P, 2, BANK], F32)) for s in range(2)]
        counted = sem(f"{use}_counted")
        cleared = sem(f"{use}_cleared")
        indexed = sem(f"{use}_indexed")
        gathered = [sem(f"{use}_gathered{s}") for s in range(BODY)]
        matched = sem(f"{use}_matched")
        summed = sem(f"{use}_summed")
        added = sem(f"{use}_added")
        block = ctx.enter_context(nc.Block())

        def turns(eng, body):
            body(0)
            with eng.Fori(1, NT // BODY) as i:
                body(i)

        @block.scalar
        def _(eng):
            def body(i):
                for h in range(2):
                    wait_if(eng, summed, BODY * i - BODY + HALF * (h + 1))
                    eng.activation(index[h][:, :], rows[:, bass.ds(BODY * i + HALF * h, HALF)],
                                   ACT.Copy).then_inc(indexed, 1)
            turns(eng, body)

        @block.gpsimd
        def _(eng):
            eng.memset(ring[:, :, D:ACCW], 1.0).then_inc(counted, 1)

            def body(i):
                for s in range(BODY):
                    if s % HALF == 0:
                        eng.wait_ge(indexed, 2 * i + s // HALF + 1)
                    if not isinstance(i, int):
                        eng.wait_ge(summed, BODY * i - BODY + s + 1)
                        eng.sem_inc(cleared, 1)
                    eng.indirect_dma_start(ring[:, s, 0:D], None, table, bass.IndirectOffsetOnAxis(
                        ap=index[s // HALF][:, s % HALF:s % HALF + 1], axis=0)).then_inc(gathered[s], 16)
            turns(eng, body)

        @block.vector
        def _(eng):
            def add(g, q):
                w = eng.value_load(b.wbase[0:1, bass.ds(g, 1)], min_val=0, max_val=NW - 2)
                eng.wait_ge(summed, (g + 1) * GROUP)
                wait_if(eng, added, g)
                eng.tensor_tensor(b.acc[:, bass.ds(w, 2), :], b.acc[:, bass.ds(w, 2), :],
                                  sums[q][:, :, 0:ACCW], ALU.add).then_inc(added, 1)

            def body(i):
                for s in range(BODY):
                    wait_if(eng, summed, BODY * i + s - ONEHOTS + 1)
                    eng.tensor_scalar(onehot[s % ONEHOTS][:, :], b.ramp[:, :],
                                      b.edst[:, bass.ds(BODY * i + s, 1)], None,
                                      ALU.is_equal).then_inc(matched, 1)
                    if s % GROUP == 1:
                        g = (BODY // GROUP) * i + s // GROUP - 1
                        if not isinstance(g, int) or g >= 0:
                            add(g, (s // GROUP - 1) % 2)
            turns(eng, body)
            add(NG - 1, (NG - 1) % 2)
            eng.wait_ge(added, NG)

        @block.tensor
        def _(eng):
            eng.wait_ge(counted, 1)

            def body(i):
                for s in range(BODY):
                    q = s // GROUP % 2
                    if s % GROUP == 0:
                        wait_if(eng, added, (BODY // GROUP) * i + s // GROUP - 1)
                    eng.wait_ge(matched, BODY * i + s + 1)
                    eng.wait_ge(gathered[s], 16 * (i + 1))
                    for half in range(2):
                        mm = eng.matmul(sums[q][:, half, 0:ACCW],
                                        onehot[s % ONEHOTS][:, half * P:(half + 1) * P], ring[:, s, :],
                                        start=(s % GROUP == 0), stop=(s % GROUP == GROUP - 1))
                    mm.then_inc(summed, 1)
            turns(eng, body)


def far_edges(nc, b, table, rows, use):
    with Phase(nc) as ctx:
        sem = lambda name: ctx.semaphore(name)
        sb = lambda name, shape, dt=F32: ctx.enter_context(nc.sbuf_tensor(name, shape, dt))
        got = sb(f"{use}_got", [P, ACCW])
        index = sb(f"{use}_index", [P, 1], I32)
        beyond = sb(f"{use}_beyond", [P, 1])
        shifted = sb(f"{use}_shifted", [P, 1])
        basis = sb(f"{use}_basis", [P, 1])
        onehot = sb(f"{use}_onehot", [P, P])
        sums = ctx.enter_context(nc.psum_tensor(f"{use}_sums", [P, BANK], F32))
        counted = sem(f"{use}_counted")
        indexed = sem(f"{use}_indexed")
        gathered = sem(f"{use}_gathered")
        prepared = sem(f"{use}_prepared")
        matched = sem(f"{use}_matched")
        summed = sem(f"{use}_summed")
        added = sem(f"{use}_added")
        cleared = sem(f"{use}_cleared")
        passed = sem(f"{use}_passed")
        block = ctx.enter_context(nc.Block())

        @block.gpsimd
        def _(eng):
            far = eng.value_load(b.maxspan[0:1, 0:1], min_val=-NW, max_val=2 * P)
            eng.memset(got[:, D:ACCW], 1.0).then_inc(counted, 1)
            with eng.If(far > 1):
                with eng.Fori(0, NT) as t:
                    eng.wait_ge(indexed, t + 1)
                    eng.sem_inc(cleared, 1)
                    eng.indirect_dma_start(got[:, 0:D], None, table, bass.IndirectOffsetOnAxis(
                        ap=index[:, 0:1], axis=0)).then_inc(gathered, 16)
                eng.sem_inc(cleared, 1)

        @block.vector
        def _(eng):
            far = eng.value_load(b.maxspan[0:1, 0:1], min_val=-NW, max_val=2 * P)
            with eng.If(far > 1):
                eng.sem_inc(added, 1)
                with eng.Fori(0, NT) as t:
                    eng.wait_ge(summed, t * NW + 1)
                    eng.tensor_copy(index[:, :], rows[:, bass.ds(t, 1)]).then_inc(indexed, 1)
                    eng.tensor_scalar(beyond[:, :], b.edst[:, bass.ds(t, 1)], float(2 * P), -float(NP + NOWHERE),
                                      ALU.is_lt, ALU.mult).then_inc(prepared, 1)
                    eng.wait_ge(prepared, t * 2 + 1)
                    eng.tensor_tensor(basis[:, :], beyond[:, :], b.edsti[:, bass.ds(t, 1)],
                                      ALU.add).then_inc(prepared, 1)
                    stand(eng, prepared, t * 2 + 2, passed)
                    with eng.Fori(0, NW) as w:
                        eng.wait_ge(added, t * NW + w + 1)
                        eng.tensor_tensor(shifted[:, :], basis[:, :], b.wstart[:, bass.ds(w, 1)],
                                          ALU.subtract).then_inc(matched, 1)
                        eng.wait_ge(matched, (t * NW + w) * 2 + 1)
                        eng.tensor_scalar(onehot[:, :], b.ramp[:, 0:P], shifted[:, 0:1], None,
                                          ALU.is_equal).then_inc(matched, 1)
                        eng.wait_ge(summed, t * NW + w + 2)
                        eng.tensor_tensor(b.acc[:, w, :], b.acc[:, w, :], sums[:, 0:ACCW],
                                          ALU.add).then_inc(added, 1)
                eng.wait_ge(added, NT * NW + 1)
                eng.tensor_copy(shifted[:, :], basis[:, :]).then_inc(prepared, 1)

        @block.tensor
        def _(eng):
            far = eng.value_load(b.maxspan[0:1, 0:1], min_val=-NW, max_val=2 * P)
            eng.wait_ge(counted, 1)
            eng.sem_inc(cleared, 1)
            with eng.If(far > 1):
                eng.sem_inc(summed, 1)
                with eng.Fori(0, NT) as t:
                    eng.wait_ge(gathered, 16 * (t + 1))
                    eng.sem_inc(cleared, 1)
                    with eng.Fori(0, NW) as w:
                        eng.wait_ge(matched, (t * NW + w) * 2 + 2)
                        eng.matmul(sums[:, 0:ACCW], onehot[:, :], got[:, :], start=True,
                                   stop=True).then_inc(summed, 1)
                eng.sem_inc(cleared, 1)


def add_relations(nc, b, m):
    with Phase(nc) as ctx:
        bias = ctx.enter_context(nc.sbuf_tensor("a_bias", [P, D], F32))
        loaded = ctx.semaphore("a_loaded")
        done = ctx.semaphore("a_done")
        block = ctx.enter_context(nc.Block())

        @block.sync
        def _(eng):
            eng.dma_start(bias[:, :], m["h_bias"].rearrange("(a d) -> a d", a=1).broadcast_to([P, D])).then_inc(loaded, 16)
            eng.wait_ge(loaded, 16)

        @block.vector
        def _(eng):
            v = Chain(eng, done)
            v.did(eng.tensor_scalar(b.degree[:, :], b.acc[:, :, D], 1.0, None, ALU.max))
            v.did(eng.scalar_tensor_tensor(b.x[:, :, :], b.acc[:, :, 0:D], 0.5 ** 0.5, b.x[:, :, :],
                                           ALU.mult, ALU.add))
            eng.wait_ge(loaded, 16)
            v.settled()
            v.did(eng.tensor_tensor(b.x[:, :, :], b.x[:, :, :],
                                    bias[:, :].unsqueeze(1).broadcast_to([P, NW, D]), ALU.add))
            v.settled()



def attention_inputs(nc, b, m, a):
    with Phase(nc) as ctx:
        sem = lambda name: ctx.semaphore(name)
        sb = lambda name, shape, dt=F32: ctx.enter_context(nc.sbuf_tensor(name, shape, dt))
        wgat = sb("g_wgat", [P, KH, HE])
        att = sb("g_att", [P, 2, HE])
        xn = [sb(f"g_xn{s}", [P, D]) for s in range(2)]
        xt = [sb(f"g_xt{s}", [P, KH, P]) for s in range(2)]
        weighted = sb("g_weighted", [P, NW, HE])
        bounds = sb("g_bounds", [P, 2 * HEADS])
        extremes = sb("g_extremes", [P, 2 * HEADS])
        width = sb("g_width", [P, HEADS])
        dsti = sb("g_dsti", [P, GNT], I32)
        hii = sb("g_hii", [P, GNT], I32)
        turned = [ctx.enter_context(nc.psum_tensor(f"g_turned{s}", [P, BANK], F32)) for s in range(2)]
        product = [ctx.enter_context(nc.psum_tensor(f"g_product{s}", [P, BANK], F32)) for s in range(2)]
        loaded = sem("g_loaded")
        normed = sem("g_normed")
        transposed = sem("g_transposed")
        copied = sem("g_copied")
        kept = sem("g_kept")
        multiplied = sem("g_multiplied")
        evacuated = sem("g_evacuated")
        chained = sem("g_chained")
        bounded = sem("g_bounded")
        reduced = sem("g_reduced")
        ramped = sem("g_ramped")
        block = ctx.enter_context(nc.Block())

        @block.sync
        def _(eng):
            eng.dma_start(wgat[:, :, :], m["W_gat"].rearrange("(k p) o -> p k o", p=P)).then_inc(loaded, 16)
            eng.dma_start(att[:, 0, :], m["att_src"].rearrange("(a h) e -> a (h e)", a=1).broadcast_to([P, HE])).then_inc(loaded, 16)
            eng.dma_start(att[:, 1, :], m["att_dst"].rearrange("(a h) e -> a (h e)", a=1).broadcast_to([P, HE])).then_inc(loaded, 16)
            eng.dma_start(a.isrc[:, :], m["gsrc_cols"]).then_inc(loaded, 16)
            eng.dma_start(dsti[:, :], m["gdst_cols"]).then_inc(loaded, 16)
            eng.wait_ge(loaded, 80)

        @block.gpsimd
        def _(eng):
            eng.iota(a.hiramp[:, :, :], pattern=[[1, NW], [0, SRCW]], base=0, channel_multiplier=0,
                     allow_small_or_imprecise_dtypes=True).then_inc(ramped, 1)
            eng.wait_ge(bounded, 1)
            eng.partition_all_reduce(extremes[:, :], bounds[:, :], P, RMAX).then_inc(reduced, 1)
            eng.wait_ge(reduced, 1)
            eng.wait_ge(ramped, 1)

        @block.vector
        def _(eng):
            def body(w, s):
                wait_if(eng, transposed, w - 1)
                eng.tensor_scalar(xn[s][:, :], b.x[:, w, :], b.mean[:, bass.ds(w, 1)], b.rstd[:, bass.ds(w, 1)],
                                  ALU.subtract, ALU.mult).then_inc(normed, 1)
                if isinstance(w, int) and w == 0:
                    return
                late(w - 1, 1 - s)

            def late(w, s):
                eng.wait_ge(multiplied, w + 1)
                eng.tensor_copy(a.rows[:, w, 0:HE], product[s][:, 0:HE]).then_inc(evacuated, 1)
            each_window(eng, body)
            late(NW - 1, 0)

            v = Chain(eng, chained)
            eng.wait_ge(loaded, 80)
            eng.wait_ge(evacuated, NW)
            for side, out in ((0, a.rows[:, :, HE:SRCW]), (1, a.drows[:, :, 0:HEADS])):
                v.did(eng.tensor_tensor(weighted[:, :, :], a.rows[:, :, 0:HE],
                                        att[:, side, :].unsqueeze(1).broadcast_to([P, NW, HE]), ALU.mult))
                v.settled()
                v.did(eng.tensor_reduce(out, weighted[:, :, :].rearrange("p w (h e) -> p w h e", e=EXPERTS),
                                        AX_X, ALU.add))
                v.settled()
            logits = a.rows[:, :, HE:SRCW].rearrange("p w h -> p h w")
            v.did(eng.tensor_reduce(bounds[:, 0:HEADS], logits, AX_X, ALU.max))
            v.did(eng.tensor_reduce(bounds[:, HEADS:], logits, AX_X, ALU.min))
            v.settled()
            eng.tensor_scalar(bounds[:, HEADS:], bounds[:, HEADS:], -1.0, None, ALU.mult).then_inc(bounded, 1)
            eng.wait_ge(reduced, 1)
            v.did(eng.tensor_tensor(width[:, :], extremes[:, 0:HEADS], extremes[:, HEADS:], ALU.add))
            v.did(eng.tensor_copy(a.peak[:, :, :], extremes[:, 0:HEADS].unsqueeze(1).broadcast_to([P, NW, HEADS])))
            v.settled()
            v.did(eng.tensor_reduce(width[:, 0:1], width[:, :], AX_X, ALU.max))
            v.settled()
            v.did(eng.tensor_scalar(a.wide[:, :], width[0:1, 0:1], SPREAD, None, ALU.is_gt))
            v.did(eng.tensor_scalar(a.isrc[:, :], a.isrc[:, :], float(N - 1), None, ALU.min))
            v.did(eng.tensor_scalar(a.idst[:, :], dsti[:, :], float(N - 1), None, ALU.min))
            v.did(eng.tensor_scalar(hii[:, :], dsti[:, :], 7, None, ALU.arith_shift_right))
            v.settled()
            v.did(eng.tensor_copy(a.hi[:, :], hii[:, :]))
            v.did(eng.scalar_tensor_tensor(a.lo[:, :], hii[:, :], float(-P), dsti[:, :], ALU.mult, ALU.add))
            v.settled()

        @block.tensor
        def _(eng):
            def turn(w, s):
                eng.wait_ge(normed, w + 1)
                wait_if(eng, kept, w - 1)
                eng.transpose(turned[s][:, 0:P], xn[s][:, 0:P], b.ident[:, :])
                eng.transpose(turned[s][:, P:D], xn[s][:, P:D], b.ident[:, :]).then_inc(transposed, 1)

            def body(w, s):
                if not (isinstance(w, int) and w == NW - 1):
                    turn(w + 1, 1 - s)
                eng.wait_ge(copied, w + 1)
                wait_if(eng, evacuated, w - 1)
                for k in range(KH):
                    mm = eng.matmul(product[s][:, 0:HE], xt[s][:, k, :], wgat[:, k, :],
                                    start=(k == 0), stop=(k == KH - 1))
                mm.then_inc(multiplied, 1)
            eng.wait_ge(loaded, 80)
            turn(0, 0)
            each_window(eng, body)

        @block.scalar
        def _(eng):
            def body(w, s):
                eng.wait_ge(transposed, w + 1)
                wait_if(eng, multiplied, w - 1)
                eng.activation(xt[s][:, :, :].rearrange("p k n -> p (k n)"), turned[s][:, 0:D],
                               ACT.Copy).then_inc(copied, 1)
                eng.activation(b.xt[:, :, bass.ds(w * P, P)], turned[s][:, 0:D].rearrange("p (k n) -> p k n", k=KH),
                               ACT.Copy).then_inc(kept, 1)
            each_window(eng, body)
            eng.wait_ge(kept, NW)


def far_peaks(nc, b, a):
    with Phase(nc) as ctx:
        sem = lambda name: ctx.semaphore(name)
        sb = lambda name, shape, dt=F32: ctx.enter_context(nc.sbuf_tensor(name, shape, dt))
        got = sb("q_got", [P, SRCW])
        index = sb("q_index", [P, 1], I32)
        diagonal = sb("q_diagonal", [P, HEADS + 1, P])
        across = sb("q_across", [P, HEADS + 1, P])
        target = sb("q_target", [P, 1])
        node = sb("q_node", [P, NW])
        match = sb("q_match", [P, P])
        floor = sb("q_floor", [P, P])
        masked = sb("q_masked", [P, HEADS, P])
        top = sb("q_top", [P, HEADS])
        spread = [ctx.enter_context(nc.psum_tensor(f"q_spread{s}", [P, BANK], F32)) for s in range(2)]
        numbered = sem("q_numbered")
        indexed = sem("q_indexed")
        gathered = sem("q_gathered")
        cleared = sem("q_cleared")
        laid = sem("q_laid")
        summed = sem("q_summed")
        copied = sem("q_copied")
        stepped = sem("q_stepped")
        started = sem("q_started")
        passed = sem("q_passed")
        block = ctx.enter_context(nc.Block())
        STEPS = 5 + HEADS

        @block.gpsimd
        def _(eng):
            wide = eng.value_load(a.wide[0:1, 0:1], min_val=0, max_val=1)
            eng.iota(node[:, :], pattern=[[P, NW]], base=0, channel_multiplier=1,
                     allow_small_or_imprecise_dtypes=True).then_inc(numbered, 1)
            with eng.If(wide > 0):
                with eng.Fori(0, GNT) as t:
                    eng.wait_ge(indexed, t + 1)
                    eng.sem_inc(cleared, 1)
                    eng.indirect_dma_start(got[:, :], None, a.source_rows, bass.IndirectOffsetOnAxis(
                        ap=index[:, 0:1], axis=0)).then_inc(gathered, 16)
                eng.sem_inc(cleared, 1)
            eng.memset(top[0:1, 0:1], 0.0).then_inc(cleared, 1)

        @block.vector
        def _(eng):
            wide = eng.value_load(a.wide[0:1, 0:1], min_val=0, max_val=1)
            eng.wait_ge(numbered, 1)
            with eng.If(wide > 0):
                eng.tensor_copy(a.peak[:, :, :], a.rows[:, :, HE:SRCW]).then_inc(started, 1)
                eng.wait_ge(started, 1)
                with eng.Fori(0, GNT) as t:
                    eng.tensor_copy(index[:, :], a.isrc[:, bass.ds(t, 1)]).then_inc(indexed, 1)
                    eng.scalar_tensor_tensor(target[:, :], a.hi[:, bass.ds(t, 1)], float(P),
                                             a.lo[:, bass.ds(t, 1)], ALU.mult, ALU.add).then_inc(started, 1)
                    eng.wait_ge(started, t + 2)
                    eng.wait_ge(gathered, 16 * (t + 1))
                    for h in range(HEADS + 1):
                        scale = got[:, HE + h:HE + h + 1] if h < HEADS else target[:, 0:1]
                        eng.tensor_scalar(diagonal[:, h, :], b.ident[:, :], scale, None,
                                          ALU.mult).then_inc(laid, 1)
                    eng.wait_ge(summed, t + 1)
                    eng.tensor_copy(across[:, 0:HEADS, :], spread[0][:, :].rearrange("p (h e) -> p h e", h=HEADS)).then_inc(copied, 1)
                    eng.tensor_copy(across[:, HEADS, :], spread[1][:, 0:P]).then_inc(copied, 1)
                    stand(eng, copied, 2 * (t + 1), passed)
                    with eng.Fori(0, NW) as w:
                        n = (t * NW + w) * STEPS
                        eng.tensor_scalar(match[:, :], across[:, HEADS, :], node[:, bass.ds(w, 1)], None,
                                          ALU.is_equal).then_inc(stepped, 1)
                        eng.wait_ge(stepped, n + 1)
                        eng.tensor_scalar(floor[:, :], match[:, :], 1.0, -LOWEST, ALU.subtract,
                                          ALU.mult).then_inc(stepped, 1)
                        for h in range(HEADS):
                            eng.tensor_tensor(masked[:, h, :], across[:, h, :], match[:, :],
                                              ALU.mult).then_inc(stepped, 1)
                        eng.wait_ge(stepped, n + 2 + HEADS)
                        eng.tensor_tensor(masked[:, :, :], masked[:, :, :],
                                          floor[:, :].unsqueeze(1).broadcast_to([P, HEADS, P]),
                                          ALU.add).then_inc(stepped, 1)
                        eng.wait_ge(stepped, n + 3 + HEADS)
                        eng.tensor_reduce(top[:, :], masked[:, :, :], AX_X, ALU.max).then_inc(stepped, 1)
                        eng.wait_ge(stepped, n + 4 + HEADS)
                        eng.tensor_tensor(a.peak[:, w, :], a.peak[:, w, :], top[:, :],
                                          ALU.max).then_inc(stepped, 1)
                        stand(eng, stepped, n + 5 + HEADS, passed)
                eng.tensor_copy(masked[:, 0, 0:1], top[:, 0:1]).then_inc(copied, 1)

        @block.tensor
        def _(eng):
            wide = eng.value_load(a.wide[0:1, 0:1], min_val=0, max_val=1)
            with eng.If(wide > 0):
                with eng.Fori(0, GNT) as t:
                    eng.wait_ge(laid, (HEADS + 1) * (t + 1))
                    eng.matmul(spread[0][:, :], b.ones[:, :], diagonal[:, 0:HEADS, :].rearrange("p h e -> p (h e)"),
                               start=True, stop=True)
                    eng.matmul(spread[1][:, 0:P], b.ones[:, :], diagonal[:, HEADS, :],
                               start=True, stop=True).then_inc(summed, 1)
                eng.sem_inc(cleared, 1)


def attention_rows(nc, b, a):
    with Phase(nc) as ctx:
        raised = ctx.enter_context(nc.sbuf_tensor("w_raised", [P, NW, HEADS], F32))
        done = ctx.semaphore("w_done")
        stored = ctx.semaphore("w_stored")
        block = ctx.enter_context(nc.Block())

        @block.vector
        def _(eng):
            v = Chain(eng, done)
            v.did(eng.tensor_tensor(raised[:, :, :], a.peak[:, :, :], a.drows[:, :, 0:HEADS], ALU.add))
            v.settled()
            v.did(eng.scalar_tensor_tensor(a.drows[:, :, HEADS:], raised[:, :, :], 0.2, raised[:, :, :],
                                           ALU.mult, ALU.max))

        @block.sync
        def _(eng):
            eng.dma_start(a.source_rows.rearrange("(w p) c -> p w c", p=P), a.rows[:, :, :]).then_inc(stored, 16)
            eng.wait_ge(done, 2)
            eng.dma_start(a.target_rows.rearrange("(w p) c -> p w c", p=P), a.drows[:, :, :]).then_inc(stored, 16)
            eng.wait_ge(stored, 32)


EARLY = 2
SPLIT = 25


def attention_edges(nc, b, m, a):
    HALF = GBODY // 2
    SLOTS = 4
    TURNS = GNT // GBODY
    LOADS = 16 * EARLY * (2 + NB)
    HIDE, PROJECT = 0, 6
    assert NW < TURNS and EARLY == GBODY // HALF
    with Phase(nc) as ctx:
        sem = lambda name: ctx.semaphore(name)
        sb = lambda name, shape, dt=F32: ctx.enter_context(nc.sbuf_tensor(name, shape, dt))
        index = [sb(f"t_index{h}", [P, 2, HALF], I32) for h in range(2)]
        source = sb("t_source", [P, GBODY, SRCW])
        target = sb("t_target", [P, GBODY, DSTW])
        values = sb("t_values", [P, GBODY, SRCW])
        logit = sb("t_logit", [P, 4, HALF, HEADS])
        place = [sb(f"t_place{s}", [P, P]) for s in range(SLOTS)]
        value = [sb(f"t_value{s}", [P, NW, SRCW]) for s in range(SLOTS)]
        w1 = sb("t_w1", [P, EARLY, KH, FF])
        w2 = sb("t_w2", [P, EARLY, NB, D])
        b1 = sb("t_b1", [P, EARLY * NB])
        hidden = sb("t_hidden", [P, NB, P])
        stage = sb("t_stage", [P, D])
        raw = ctx.enter_context(nc.psum_tensor("t_raw", [P, BANK], F32))
        out = ctx.enter_context(nc.psum_tensor("t_out", [P, BANK], F32))
        loaded = sem("t_loaded")
        multiplied = sem("t_multiplied")
        activated = sem("t_activated")
        projected = sem("t_projected")
        kept = sem("t_kept")
        stored = sem("t_stored")
        indexed = sem("t_indexed")
        cleared = sem("t_cleared")
        gathered = [sem(f"t_gathered{s}") for s in range(GBODY)]
        lifted = sem("t_lifted")
        weighed = sem("t_weighed")
        valued = sem("t_valued")
        built = sem("t_built")
        summed = sem("t_summed")
        block = ctx.enter_context(nc.Block())

        def turns(eng, body):
            body(0)
            with eng.Fori(1, TURNS) as i:
                body(i)

        @block.sync
        def _(eng):
            for e in range(EARLY):
                eng.dma_start(w1[:, e, :, :], m["W1"][e].rearrange("(k p) f -> p k f", p=P)).then_inc(loaded, 16)
                eng.dma_start(w2[:, e, :, :], m["W2"][e].rearrange("(j p) d -> p j d", p=P)).then_inc(loaded, 16)
                for j in range(NB):
                    eng.dma_start(b1[:, e * NB + j:e * NB + j + 1],
                                  m["b1"][e:e + 1, j * P:(j + 1) * P].rearrange("a p -> p a")).then_inc(loaded, 16)
            eng.wait_ge(loaded, LOADS)
            eng.sem_inc(stored, 16)
            first = a.first.rearrange("e (w p) d -> e w p d", p=P)
            with eng.Fori(0, NW) as w:
                for e in range(EARLY):
                    eng.wait_ge(kept, EARLY * w + e + 1)
                    eng.dma_start(first[e, w], stage[:, :]).then_inc(stored, 16)
            eng.wait_ge(stored, 16 * (EARLY * NW + 1))

        @block.gpsimd
        def _(eng):
            def body(i):
                for s in range(GBODY):
                    h = s // HALF
                    if s % HALF == 0:
                        eng.wait_ge(indexed, 4 * i + 2 * h + 2)
                        eng.sem_inc(cleared, 1)
                        if not isinstance(i, int):
                            eng.wait_ge(valued, 2 * i - 1 + h)
                            eng.sem_inc(cleared, 1)
                    eng.indirect_dma_start(source[:, s, :], None, a.source_rows, bass.IndirectOffsetOnAxis(
                        ap=index[h][:, 0, s % HALF:s % HALF + 1], axis=0)).then_inc(gathered[s], 16)
                    eng.indirect_dma_start(target[:, s, :], None, a.target_rows, bass.IndirectOffsetOnAxis(
                        ap=index[h][:, 1, s % HALF:s % HALF + 1], axis=0)).then_inc(gathered[s], 16)
            turns(eng, body)

        @block.scalar
        def _(eng):
            def copy(i, h):
                wait_if(eng, valued, 2 * i - 1 + h)
                eng.activation(index[h][:, 0, :], a.isrc[:, bass.ds(GBODY * i + HALF * h, HALF)],
                               ACT.Copy).then_inc(indexed, 1)
                eng.activation(index[h][:, 1, :], a.idst[:, bass.ds(GBODY * i + HALF * h, HALF)],
                               ACT.Copy).then_inc(indexed, 1)

            def weigh(i, h):
                eng.wait_ge(lifted, (2 * i + h + 1) * 4)
                wait_if(eng, built, GBODY * i - GBODY + HALF * (h + 1))
                eng.activation(values[:, h * HALF:(h + 1) * HALF, HE:SRCW], logit[:, 3, :, :],
                               ACT.Exp).then_inc(weighed, 1)

            def activate(w, e):
                eng.wait_ge(multiplied, EARLY * w + e + 1)
                for j in range(NB):
                    act = eng.activation(hidden[:, j, :], raw[:, j * P:(j + 1) * P], ACT.Gelu, bias=b1[:, e * NB + j:e * NB + j + 1])
                act.then_inc(activated, 1)

            def keep(w, e):
                eng.wait_ge(projected, EARLY * w + e + 1)
                eng.wait_ge(stored, 16 * (EARLY * w + e + 1))
                eng.activation(stage[:, :], out[:, 0:D], ACT.Copy).then_inc(kept, 1)

            copy(0, 0)
            copy(0, 1)
            weigh(0, 0)
            eng.wait_ge(loaded, LOADS)
            with eng.Fori(1, NW + 1) as i:
                copy(i, 0)
                activate(i - 1, 0)
                weigh(i - 1, 1)
                keep(i - 1, 0)
                copy(i, 1)
                activate(i - 1, 1)
                weigh(i, 0)
                keep(i - 1, 1)
            with eng.Fori(NW + 1, TURNS) as i:
                copy(i, 0)
                weigh(i - 1, 1)
                copy(i, 1)
                weigh(i, 0)
            weigh(TURNS - 1, 1)
            eng.wait_ge(kept, EARLY * NW)

        @block.vector
        def _(eng):
            def half_turn(i, h):
                half = slice(h * HALF, (h + 1) * HALF)
                n = (2 * i + h) * 4
                for s in range(h * HALF, (h + 1) * HALF):
                    eng.wait_ge(gathered[s], 32 * (i + 1))
                wait_if(eng, weighed, 2 * i + h)
                eng.tensor_tensor(logit[:, 0, :, :], source[:, half, HE:SRCW], target[:, half, 0:HEADS],
                                  ALU.add).then_inc(lifted, 1)
                eng.wait_ge(lifted, n + 1)
                eng.scalar_tensor_tensor(logit[:, 1, :, :], logit[:, 0, :, :], 0.2, logit[:, 0, :, :],
                                         ALU.mult, ALU.max).then_inc(lifted, 1)
                eng.wait_ge(lifted, n + 2)
                eng.tensor_tensor(logit[:, 2, :, :], logit[:, 1, :, :], target[:, half, HEADS:],
                                  ALU.subtract).then_inc(lifted, 1)
                eng.wait_ge(lifted, n + 3)
                eng.tensor_scalar(logit[:, 3, :, :], logit[:, 2, :, :], 0.0, None,
                                  ALU.min).then_inc(lifted, 1)
                eng.wait_ge(weighed, 2 * i + h + 1)
                eng.tensor_tensor(values[:, half, 0:HE].rearrange("p t (h e) -> p t h e", e=EXPERTS),
                                  source[:, half, 0:HE].rearrange("p t (h e) -> p t h e", e=EXPERTS),
                                  values[:, half, HE:SRCW].unsqueeze(3).broadcast_to([P, HALF, HEADS, EXPERTS]),
                                  ALU.mult).then_inc(valued, 1)
                eng.wait_ge(valued, 2 * i + h + 1)
                for s in range(h * HALF, (h + 1) * HALF):
                    t = GBODY * i + s
                    wait_if(eng, summed, t - SLOTS + 1)
                    eng.tensor_scalar(place[s % SLOTS][:, :], b.ramp[:, 0:P], a.lo[:, bass.ds(t, 1)], None,
                                      ALU.is_equal)
                    eng.scalar_tensor_tensor(value[s % SLOTS][:, :, :], a.hiramp[:, :, :], a.hi[:, bass.ds(t, 1)],
                                             values[:, s, :].unsqueeze(1).broadcast_to([P, NW, SRCW]),
                                             ALU.is_equal, ALU.mult).then_inc(built, 1)

            def body(i):
                half_turn(i, 0)
                half_turn(i, 1)
            turns(eng, body)

        @block.tensor
        def _(eng):
            def hide(w, e):
                wait_if(eng, activated, EARLY * w + e)
                for j in range(NB):
                    for k in range(KH):
                        mm = eng.matmul(raw[:, j * P:(j + 1) * P], w1[:, e, k, j * P:(j + 1) * P],
                                        b.xt[:, k, bass.ds(w * P, P)], start=(k == 0), stop=(k == KH - 1))
                mm.then_inc(multiplied, 1)

            def project(w, e):
                eng.wait_ge(activated, EARLY * w + e + 1)
                wait_if(eng, kept, EARLY * w + e)
                for j in range(NB):
                    mm = eng.matmul(out[:, 0:D], hidden[:, j, :], w2[:, e, j, :],
                                    start=(j == 0), stop=(j == NB - 1))
                mm.then_inc(projected, 1)

            def body(i, expert):
                for s in range(GBODY):
                    first = isinstance(i, int) and s == 0
                    eng.wait_ge(built, GBODY * i + s + 1)
                    for c, (lo, hi) in enumerate(((0, SPLIT), (SPLIT, NW))):
                        mm = eng.matmul(a.sums[c][:, 0:(hi - lo) * SRCW], place[s % SLOTS][:, :],
                                        value[s % SLOTS][:, lo:hi, :].rearrange("p w c -> p (w c)"),
                                        start=first, stop=False, skip_group_check=True)
                    mm.then_inc(summed, 1)
                    if first:
                        eng.wait_ge(loaded, LOADS)
                    if expert and s % HALF == HIDE:
                        hide(i, s // HALF)
                    if expert and s % HALF == PROJECT:
                        project(i, s // HALF)
            body(0, True)
            with eng.Fori(1, NW) as i:
                body(i, True)
            with eng.Fori(NW, TURNS) as i:
                body(i, False)


def gates(nc, b, m, a):
    with Phase(nc) as ctx:
        sb = lambda name, shape, dt=F32: ctx.enter_context(nc.sbuf_tensor(name, shape, dt))
        sem = lambda name: ctx.semaphore(name)
        own = sb("s_own", [P, 3, NW, HEADS])
        sums = sb("s_sums", [P, NW, SRCW])
        params = sb("s_params", [P, 3, HE])
        mixed = sb("s_mixed", [P, NW, HE])
        squared = sb("s_squared", [P, NW, HE])
        stat = sb("s_stat", [P, 4, NW])
        score = sb("s_score", [P, NW, EXPERTS])
        rank = sb("s_rank", [P, NW, EXPERTS])
        beaten = sb("s_beaten", [P, EXPERTS * (EXPERTS - 1), NW])
        loaded = sem("s_loaded")
        chained = sem("s_chained")
        weighed = sem("s_weighed")
        asked = sem("s_asked")
        block = ctx.enter_context(nc.Block())

        @block.sync
        def _(eng):
            for n, source in enumerate((m["b_gat"], m["ln_gamma"], m["ln_beta"])):
                eng.dma_start(params[:, n, :], source.rearrange("(a d) -> a d", a=1).broadcast_to([P, HE])).then_inc(loaded, 16)
            eng.wait_ge(loaded, 48)

        @block.scalar
        def _(eng):
            eng.wait_ge(asked, 1)
            eng.activation(own[:, 2, :, :], own[:, 1, :, :], ACT.Exp).then_inc(weighed, 1)
            eng.wait_ge(asked, 2)
            eng.activation(stat[:, 2, :], stat[:, 1, :], ACT.Sqrt).then_inc(weighed, 1)
            eng.wait_ge(asked, 3)
            eng.activation(score[:, :, :], score[:, :, :], ACT.Exp).then_inc(weighed, 1)

        @block.vector
        def _(eng):
            v = Chain(eng, chained)

            def step(instruction):
                v.did(instruction)
                v.settled()

            wide = lambda t: t.unsqueeze(2).broadcast_to([P, NW, HE])
            param = lambda n: params[:, n, :].unsqueeze(1).broadcast_to([P, NW, HE])
            step(eng.tensor_tensor(own[:, 0, :, :], a.rows[:, :, HE:SRCW], a.drows[:, :, 0:HEADS], ALU.add))
            step(eng.scalar_tensor_tensor(own[:, 1, :, :], own[:, 0, :, :], 0.2, own[:, 0, :, :],
                                          ALU.mult, ALU.max))
            step(eng.tensor_copy(sums[:, 0:SPLIT, :].rearrange("p w c -> p (w c)"), a.sums[0][:, 0:SPLIT * SRCW]))
            step(eng.tensor_copy(sums[:, SPLIT:, :].rearrange("p w c -> p (w c)"), a.sums[1][:, 0:(NW - SPLIT) * SRCW]))
            eng.tensor_tensor(own[:, 1, :, :], own[:, 1, :, :], a.drows[:, :, HEADS:], ALU.subtract).then_inc(asked, 1)
            eng.wait_ge(weighed, 1)
            step(eng.tensor_tensor(mixed[:, :, :].rearrange("p w (h e) -> p w h e", e=EXPERTS),
                                   a.rows[:, :, 0:HE].rearrange("p w (h e) -> p w h e", e=EXPERTS),
                                   own[:, 2, :, :].unsqueeze(3).broadcast_to([P, NW, HEADS, EXPERTS]), ALU.mult))
            step(eng.tensor_tensor(mixed[:, :, :], mixed[:, :, :], sums[:, :, 0:HE], ALU.add))
            step(eng.tensor_tensor(own[:, 0, :, :], own[:, 2, :, :], sums[:, :, HE:SRCW], ALU.add))
            step(eng.tensor_scalar(own[:, 0, :, :], own[:, 0, :, :], 1e-16, None, ALU.add))
            step(eng.reciprocal(own[:, 1, :, :], own[:, 0, :, :]))
            step(eng.tensor_tensor(mixed[:, :, :].rearrange("p w (h e) -> p w h e", e=EXPERTS),
                                   mixed[:, :, :].rearrange("p w (h e) -> p w h e", e=EXPERTS),
                                   own[:, 1, :, :].unsqueeze(3).broadcast_to([P, NW, HEADS, EXPERTS]), ALU.mult))
            eng.wait_ge(loaded, 48)
            step(eng.tensor_tensor(mixed[:, :, :], mixed[:, :, :], param(0), ALU.add))
            step(eng.tensor_reduce(stat[:, 0, :], mixed[:, :, :], AX_X, ALU.add))
            step(eng.tensor_scalar(stat[:, 0, :], stat[:, 0, :], 1.0 / HE, None, ALU.mult))
            step(eng.tensor_tensor(mixed[:, :, :], mixed[:, :, :], wide(stat[:, 0, :]), ALU.subtract))
            step(eng.tensor_tensor(squared[:, :, :], mixed[:, :, :], mixed[:, :, :], ALU.mult))
            step(eng.tensor_reduce(stat[:, 1, :], squared[:, :, :], AX_X, ALU.add))
            eng.tensor_scalar(stat[:, 1, :], stat[:, 1, :], 1.0 / HE, EPS, ALU.mult, ALU.add).then_inc(asked, 1)
            eng.wait_ge(weighed, 2)
            step(eng.reciprocal(stat[:, 3, :], stat[:, 2, :]))
            step(eng.tensor_tensor(mixed[:, :, :], mixed[:, :, :], wide(stat[:, 3, :]), ALU.mult))
            step(eng.tensor_tensor(mixed[:, :, :], mixed[:, :, :], param(1), ALU.mult))
            step(eng.tensor_tensor(mixed[:, :, :], mixed[:, :, :], param(2), ALU.add))
            step(eng.tensor_reduce(score[:, :, :], mixed[:, :, :].rearrange("p w (h e) -> p w e h", e=EXPERTS),
                                   AX_X, ALU.add))
            step(eng.tensor_scalar(score[:, :, :], score[:, :, :], 1.0 / HEADS, None, ALU.mult))
            n = 0
            for i in range(EXPERTS):
                for j in range(EXPERTS):
                    if i != j:
                        v.did(eng.tensor_tensor(beaten[:, n, :], score[:, :, j], score[:, :, i],
                                                ALU.is_ge if j < i else ALU.is_gt))
                        n += 1
            v.did(eng.tensor_reduce(stat[:, 0, :], score[:, :, :], AX_X, ALU.max))
            v.settled()
            step(eng.tensor_reduce(rank[:, :, :].rearrange("p w e -> p e w"),
                                   beaten[:, :, :].rearrange("p (i j) w -> p i w j", i=EXPERTS), AX_X, ALU.add))
            eng.tensor_tensor(score[:, :, :], score[:, :, :],
                              stat[:, 0, :].unsqueeze(2).broadcast_to([P, NW, EXPERTS]),
                              ALU.subtract).then_inc(asked, 1)
            eng.wait_ge(weighed, 3)
            step(eng.scalar_tensor_tensor(score[:, :, :], rank[:, :, :], 1.5, score[:, :, :], ALU.is_lt, ALU.mult))
            step(eng.tensor_reduce(stat[:, 0, :], score[:, :, :], AX_X, ALU.add))
            step(eng.reciprocal(stat[:, 1, :], stat[:, 0, :]))
            step(eng.tensor_tensor(a.gate[:, :, :], score[:, :, :],
                                   stat[:, 1, :].unsqueeze(2).broadcast_to([P, NW, EXPERTS]), ALU.mult))



CHUNK = 512
CHUNKS = NP // CHUNK
CW = CHUNK // P


def experts(nc, b, m, a):
    LATE = EXPERTS - EARLY
    STEPS = 2 * EARLY
    with Phase(nc) as ctx:
        sem = lambda name: ctx.semaphore(name)
        sb = lambda name, shape, dt=F32: ctx.enter_context(nc.sbuf_tensor(name, shape, dt))
        w1 = sb("m_w1", [P, LATE, KH, FF])
        w2 = sb("m_w2", [P, LATE, NB, D])
        b1 = sb("m_b1", [P, EXPERTS * NB])
        b1rows = sb("m_b1rows", [EXPERTS * NB, P])
        b2 = sb("m_b2", [P, EXPERTS, D])
        first = sb("m_first", [P, EARLY, CW, D])
        hidden = [sb(f"m_hidden{s}", [P, NB, CHUNK]) for s in range(LATE)]
        raw = [ctx.enter_context(nc.psum_tensor(f"m_raw{s}", [P, BANK], F32)) for s in range(4)]
        out = [ctx.enter_context(nc.psum_tensor(f"m_out{s}", [P, BANK], F32)) for s in range(3)]
        turned = ctx.enter_context(nc.psum_tensor("m_turned", [P, BANK], F32))
        loaded = sem("m_loaded")
        b1turned = sem("m_b1turned")
        b1kept = sem("m_b1kept")
        multiplied = sem("m_multiplied")
        activated = sem("m_activated")
        projected = sem("m_projected")
        added = sem("m_added")
        biased = sem("m_biased")
        fetched = sem("m_fetched")
        shared = sem("m_shared")
        block = ctx.enter_context(nc.Block())
        WAYS = 2

        def chunks(body):
            def run(eng):
                body(eng, 0, CW)
                with eng.Fori(1, CHUNKS) as c:
                    body(eng, c, CW)
                body(eng, CHUNKS, NW - CHUNKS * CW)
            return run

        @block.sync
        def _(eng):
            for e in range(LATE):
                eng.dma_start(w1[:, e, :, :], m["W1"][EARLY + e].rearrange("(k p) f -> p k f", p=P)).then_inc(loaded, 16)
                eng.dma_start(w2[:, e, :, :], m["W2"][EARLY + e].rearrange("(j p) d -> p j d", p=P)).then_inc(loaded, 16)
            eng.dma_start(b1rows[:, :], m["b1"].rearrange("e (j p) -> (e j) p", p=P)).then_inc(loaded, 16)
            eng.dma_start(b2[:, :, :].rearrange("p e d -> p (e d)"),
                          m["b2"].rearrange("(a e) d -> a (e d)", a=1).broadcast_to([P, EXPERTS * D])).then_inc(loaded, 16)
            eng.wait_ge(loaded, 16 * (2 * LATE + 2))

            def fetch(eng, c, blocks):
                wait_if(eng, shared, STEPS * CW * c)
                for e in range(EARLY):
                    eng.dma_start(first[:, e, 0:blocks, :], a.first[e, bass.ds(c * CHUNK, blocks * P), :].rearrange(
                        "(q p) d -> p q d", p=P)).then_inc(fetched, 16)
            chunks(fetch)(eng)
            eng.wait_ge(fetched, 16 * EARLY * (CHUNKS + 1))

        @block.tensor
        def _(eng):
            eng.wait_ge(loaded, 16 * (2 * LATE + 2))
            eng.transpose(turned[:, 0:EXPERTS * NB], b1rows[:, :], b.ident[0:EXPERTS * NB, 0:EXPERTS * NB]).then_inc(b1turned, 1)

            def hide(c, e, blocks):
                for j in range(NB):
                    n = (LATE * c + e) * NB + j
                    wait_if(eng, activated, n - 3)
                    for k in range(KH):
                        mm = eng.matmul(raw[j][:, 0:blocks * P], w1[:, e, k, j * P:(j + 1) * P],
                                        b.xt[:, k, bass.ds(c * CHUNK, blocks * P)],
                                        start=(k == 0), stop=(k == KH - 1))
                    mm.then_inc(multiplied, 1)

            def project(c, e, blocks):
                eng.wait_ge(activated, (LATE * c + e + 1) * NB)
                for q in range(blocks):
                    n = (LATE * c + e) * CW + q if blocks == CW else LATE * CHUNKS * CW + e * blocks + q
                    wait_if(eng, added, n - 1)
                    place = out[(q if blocks == CW else e) % WAYS]
                    for j in range(NB):
                        mm = eng.matmul(place[:, 0:D], hidden[e][:, j, q * P:(q + 1) * P], w2[:, e, j, :],
                                        start=(j == 0), stop=(j == NB - 1))
                    mm.then_inc(projected, 1)

            def body(eng, c, blocks):
                hide(c, 0, blocks)
                for e in range(LATE):
                    if e + 1 < LATE:
                        hide(c, e + 1, blocks)
                    project(c, e, blocks)
            chunks(body)(eng)

        @block.scalar
        def _(eng):
            eng.wait_ge(b1turned, 1)
            eng.activation(b1[:, :], turned[:, 0:EXPERTS * NB], ACT.Copy).then_inc(b1kept, 1)
            eng.wait_ge(b1kept, 1)

            def body(eng, c, blocks):
                for e in range(LATE):
                    if blocks == CW:
                        wait_if(eng, projected, (LATE * c + e - 1) * CW)
                    else:
                        eng.wait_ge(projected, LATE * CHUNKS * CW + (e - 1) * blocks if e > 1
                                    else (LATE * CHUNKS + e - 1) * CW if e == 0 else LATE * CHUNKS * CW)
                    for j in range(NB):
                        eng.wait_ge(multiplied, (LATE * c + e) * NB + j + 1)
                        eng.activation(hidden[e][:, j, 0:blocks * P], raw[j][:, 0:blocks * P], ACT.Gelu,
                                       bias=b1[:, (EARLY + e) * NB + j:(EARLY + e) * NB + j + 1]).then_inc(activated, 1)
            chunks(body)(eng)

        @block.vector
        def _(eng):
            def body(eng, c, blocks):
                for e in range(LATE):
                    for q in range(blocks):
                        n = (LATE * c + e) * CW + q if blocks == CW else LATE * CHUNKS * CW + e * blocks + q
                        w = CW * c + q
                        if e:
                            eng.wait_ge(added, n - blocks + 1)
                        eng.scalar_tensor_tensor(b.x[:, w, :], b2[:, EARLY + e, :], a.gate[:, w, EARLY + e:EARLY + e + 1], b.x[:, w, :],
                                                 ALU.mult, ALU.add).then_inc(biased, 1)
                        eng.wait_ge(projected, n + 1)
                        eng.wait_ge(biased, n + 1)
                        eng.scalar_tensor_tensor(b.x[:, w, :], out[(q if blocks == CW else e) % WAYS][:, 0:D],
                                                 a.gate[:, w, EARLY + e:EARLY + e + 1], b.x[:, w, :],
                                                 ALU.mult, ALU.add).then_inc(added, 1)
                for e in range(EARLY):
                    for q in range(blocks):
                        w = CW * c + q
                        n = STEPS * CW * c + 2 * (e * blocks + q)
                        if e:
                            eng.wait_ge(shared, n - 2 * blocks + 2)
                        else:
                            eng.wait_ge(added, LATE * CW * c + (LATE - 1) * blocks + q + 1)
                        eng.scalar_tensor_tensor(b.x[:, w, :], b2[:, e, :], a.gate[:, w, e:e + 1], b.x[:, w, :],
                                                 ALU.mult, ALU.add).then_inc(shared, 1)
                        eng.wait_ge(shared, n + 1)
                        eng.wait_ge(fetched, 16 * EARLY * (c + 1))
                        eng.scalar_tensor_tensor(b.x[:, w, :], first[:, e, q, :], a.gate[:, w, e:e + 1],
                                                 b.x[:, w, :], ALU.mult, ALU.add).then_inc(shared, 1)
            eng.wait_ge(loaded, 16 * (2 * LATE + 2))
            chunks(body)(eng)
            eng.wait_ge(shared, STEPS * NW)
            eng.wait_ge(added, LATE * NW)



def sparse_table(nc, b, m):
    ROUNDS = 32 // 8
    GROUP4 = 4
    WAYS = 2 * GROUP4
    assert NW % WAYS == 1 and ROUNDS == GROUP4

    def each_few(eng, body):
        body([(q, q) for q in range(WAYS)])
        with eng.Fori(1, NW // WAYS) as i:
            body([(WAYS * i + q, q) for q in range(WAYS)])
        body([(NW - 1, 0)])

    with Phase(nc) as ctx:
        sem = lambda name: ctx.semaphore(name)
        sb = lambda name, shape, dt=F32: ctx.enter_context(nc.sbuf_tensor(name, shape, dt))
        weights = sb("n_weights", [P, KH, 2, D])
        xn = [sb(f"n_xn{s}", [P, D]) for s in range(2)]
        xt = [sb(f"n_xt{s}", [P, KH, P]) for s in range(2)]
        full = [sb(f"n_full{s}", [P, 2, D]) for s in range(WAYS)]
        left = [sb(f"n_left{s}", [P, D]) for s in range(WAYS)]
        best = [sb(f"n_best{s}", [P, 8]) for s in range(WAYS)]
        sparse = [sb(f"n_sparse{s}", [P, D]) for s in range(WAYS)]
        turned = [ctx.enter_context(nc.psum_tensor(f"n_turned{s}", [P, BANK], F32)) for s in range(2)]
        product = [ctx.enter_context(nc.psum_tensor(f"n_product{s}", [P, BANK], F32)) for s in range(2)]
        loaded = sem("n_loaded")
        normed = sem("n_normed")
        transposed = sem("n_transposed")
        copied = sem("n_copied")
        multiplied = sem("n_multiplied")
        evacuated = sem("n_evacuated")
        picked = [sem(f"n_picked{s}") for s in range(WAYS)]
        passed = sem("n_passed")
        chosen = sem("n_chosen")
        added = sem("n_added")
        cleared = sem("n_cleared")
        stored = [sem(f"n_stored{s}") for s in range(WAYS)]
        block = ctx.enter_context(nc.Block())
        table = m["table2"].rearrange("(w p) d -> w p d", p=P)

        @block.sync
        def _(eng):
            for n, source in enumerate((m["W_self"], m["W_neigh"])):
                eng.dma_start(weights[:, :, n, :], source.rearrange("(k p) d -> p k d", p=P)).then_inc(loaded, 16)

            def body(few):
                for w, q in few:
                    eng.wait_ge(chosen, w + 1)
                    eng.dma_start(table[w], sparse[q][:, :]).then_inc(stored[q], 16)
            each_few(eng, body)
            for q in range(WAYS):
                eng.wait_ge(stored[q], 16 * (NW // WAYS + (q == 0)))
            eng.wait_ge(loaded, 32)

        @block.gpsimd
        def _(eng):
            eng.memset(b.acc[:, :, :], 0.0).then_inc(cleared, 1)
            eng.wait_ge(cleared, 1)

        @block.vector
        def _(eng):
            def norm(w, s):
                wait_if(eng, transposed, w - 1)
                eng.tensor_scalar(xn[s][:, :], b.x[:, w, :], b.mean[:, bass.ds(w, 1)], b.rstd[:, bass.ds(w, 1)],
                                  ALU.subtract, ALU.mult).then_inc(normed, 1)

            def add(w, q):
                eng.wait_ge(evacuated, w + 1)
                eng.wait_ge(normed, w + 1)
                eng.tensor_tensor(b.x[:, w, :], b.x[:, w, :], full[q][:, 0, :], ALU.add).then_inc(added, 1)

            def search(few, following):
                earlier = lambda w, q: (w - q) * (2 * ROUNDS // WAYS)
                for r in range(ROUNDS):
                    values = lambda q: full[q][:, 1, :] if r == 0 else left[q][:, :]
                    if r < len(following):
                        w, q = following[r]
                        if not (isinstance(w, int) and w == NW - 1):
                            norm(w + 1, (q + 1) % 2)
                    for w, q in few:
                        stand(eng, picked[q], earlier(w, q) + 2 * r, passed)
                        eng.max(best[q][:, :], values(q)).then_inc(picked[q], 1)
                    for w, q in few:
                        stand(eng, picked[q], earlier(w, q) + 2 * r + 1, passed)
                        eng.match_replace(left[q][:, :], best[q][:, :], values(q), LOWEST).then_inc(picked[q], 1)
                    if r < len(following):
                        add(*following[r])
                for w, q in few:
                    eng.wait_ge(picked[q], earlier(w, q) + 2 * ROUNDS)
                    if not isinstance(w, int) or w >= WAYS:
                        eng.wait_ge(stored[q], (w - q) * (16 // WAYS))
                    eng.scalar_tensor_tensor(sparse[q][:, :], left[q][:, :], LOWEST, full[q][:, 1, :],
                                             ALU.is_equal, ALU.mult).then_inc(chosen, 1)

            def pair(i):
                here = lambda low: [(WAYS * i + q, q % WAYS) for q in range(low, low + GROUP4)
                                    if not isinstance(i, int) or WAYS * i + q < NW]
                search(here(0), here(GROUP4))
                search(here(GROUP4), here(WAYS))

            norm(0, 0)
            for w in range(GROUP4):
                norm(w + 1, (w + 1) % 2)
                add(w, w)
            pair(0)
            with eng.Fori(1, NW // WAYS - 1) as i:
                pair(i)
            pair(NW // WAYS - 1)
            search([(NW - 1, 0)], [])
            eng.wait_ge(added, NW)
            eng.wait_ge(chosen, NW)

        @block.tensor
        def _(eng):
            def turn(w, s):
                eng.wait_ge(normed, w + 1)
                wait_if(eng, copied, w - 1)
                eng.transpose(turned[s][:, 0:P], xn[s][:, 0:P], b.ident[:, :])
                eng.transpose(turned[s][:, P:D], xn[s][:, P:D], b.ident[:, :]).then_inc(transposed, 1)

            def body(w, s):
                if not (isinstance(w, int) and w == NW - 1):
                    turn(w + 1, 1 - s)
                eng.wait_ge(copied, w + 1)
                wait_if(eng, evacuated, w - 1)
                for k in range(KH):
                    mm = eng.matmul(product[s][:, :], xt[s][:, k, :],
                                    weights[:, k, :, :].rearrange("p n d -> p (n d)"),
                                    start=(k == 0), stop=(k == KH - 1))
                mm.then_inc(multiplied, 1)
            eng.wait_ge(loaded, 32)
            turn(0, 0)
            each_window(eng, body)

        @block.scalar
        def _(eng):
            def copy(w, s):
                eng.wait_ge(transposed, w + 1)
                wait_if(eng, multiplied, w - 1)
                eng.activation(xt[s][:, :, :].rearrange("p k n -> p (k n)"), turned[s][:, 0:D],
                               ACT.Copy).then_inc(copied, 1)

            def body(few):
                for w, q in few:
                    if not (isinstance(w, int) and w == NW - 1):
                        copy(w + 1, (q + 1) % 2)
                    eng.wait_ge(multiplied, w + 1)
                    wait_if(eng, chosen, w - WAYS + 1)
                    eng.activation(full[q][:, :, :].rearrange("p n d -> p (n d)"), product[q % 2][:, :],
                                   ACT.Copy).then_inc(evacuated, 1)
            copy(0, 0)
            each_few(eng, body)


def add_neighbours(nc, b):
    with Phase(nc) as ctx:
        share = ctx.enter_context(nc.sbuf_tensor("d_share", [P, NW], F32))
        done = ctx.semaphore("d_done")
        block = ctx.enter_context(nc.Block())

        @block.vector
        def _(eng):
            v = Chain(eng, done)
            v.did(eng.reciprocal(share[:, :], b.degree[:, :]))
            v.settled()
            v.did(eng.tensor_tensor(b.acc[:, :, 0:D], b.acc[:, :, 0:D],
                                    share[:, :].unsqueeze(2).broadcast_to([P, NW, D]), ALU.mult))
            v.settled()
            v.did(eng.tensor_tensor(b.x[:, :, :], b.x[:, :, :], b.acc[:, :, 0:D], ALU.add))
            v.settled()


def attention_phase(nc, b, m):
    with Phase(nc) as ctx:
        sb = lambda name, shape, dt=F32: ctx.enter_context(nc.sbuf_tensor(name, shape, dt))
        a = Named()
        a.rows = sb("rows", [P, NW, SRCW])
        a.drows = sb("drows", [P, NW, DSTW])
        a.peak = sb("peak", [P, NW, HEADS])
        a.gate = sb("gate", [P, NW, EXPERTS])
        a.wide = sb("wide", [1, 1], I32)
        a.first = nc.dram_tensor("first_outputs", [EARLY, NP, D], F32).ap()
        a.source_rows = nc.dram_tensor("source_rows", [NP, SRCW], F32).ap()
        a.target_rows = nc.dram_tensor("target_rows", [NP, DSTW], F32).ap()
        with ExitStack() as edges:
            eb = lambda name, shape, dt=F32: edges.enter_context(nc.sbuf_tensor(name, shape, dt))
            a.isrc = eb("isrc", [P, GNT], I32)
            a.idst = eb("idst", [P, GNT], I32)
            a.hi = eb("hi", [P, GNT])
            a.lo = eb("lo", [P, GNT])
            a.hiramp = eb("hiramp", [P, NW, SRCW])
            attention_inputs(nc, b, m, a)
            far_peaks(nc, b, a)
            attention_rows(nc, b, a)
            a.sums = [edges.enter_context(nc.psum_tensor(f"gsums{c}", [P, BANK], F32)) for c in range(2)]
            attention_edges(nc, b, m, a)
            gates(nc, b, m, a)
        experts(nc, b, m, a)



SB = INNER // P


def slice_weights(nc, m, f):
    with Phase(nc) as ctx:
        sem = lambda name: ctx.semaphore(name)
        sb = lambda name, shape: ctx.enter_context(nc.sbuf_tensor(name, shape, F32))
        wxt = sb("l_wxt", [SD, SH, D])
        wslice = sb("l_wslice", [SD, SG])
        bx = sb("l_bx", [SD, SH])
        bslice = sb("l_bslice", [1, SG])
        heat = sb("l_heat", [P, SH])
        cool = sb("l_cool", [P, SH])
        one = sb("l_one", [1, 1])
        joined = [ctx.enter_context(nc.psum_tensor(f"l_joined{k}", [P, BANK], F32)) for k in range(KH)]
        bias = ctx.enter_context(nc.psum_tensor("l_bias", [P, BANK], F32))
        loaded = sem("l_loaded")
        multiplied = sem("l_multiplied")
        done = sem("l_done")
        block = ctx.enter_context(nc.Block())

        @block.sync
        def _(eng):
            eng.dma_start(wxt[:, :, :], m["W_xT"].rearrange("(h c) k -> c h k", c=SD)).then_inc(loaded, 16)
            eng.dma_start(wslice[:, :], m["W_slice"]).then_inc(loaded, 16)
            eng.dma_start(bx[:, :], m["b_x_cols"]).then_inc(loaded, 16)
            eng.dma_start(bslice[:, :], m["b_slice"].rearrange("(a g) -> a g", a=1)).then_inc(loaded, 16)
            eng.dma_start(heat[:, :], m["temperature"].rearrange("(a h) -> a h", a=1).broadcast_to([P, SH])).then_inc(loaded, 16)
            eng.dma_start(f.wfx[:, :, :], m["W_fx"].rearrange("(k p) o -> p k o", p=P)).then_inc(loaded, 16)
            eng.dma_start(f.bfx[:, :], m["b_fx"].rearrange("(a o) -> a o", a=1)).then_inc(loaded, 16)
            eng.dma_start(f.wout[:, :, :], m["W_out"].rearrange("(h c) d -> c h d", c=SD)).then_inc(loaded, 16)
            for n, source in enumerate((m["W_q"], m["W_k"], m["W_v"])):
                eng.dma_start(f.wqkv[:, n, :], source).then_inc(loaded, 16)
            eng.dma_start(f.bout[:, :], m["b_out"].rearrange("(a d) -> a d", a=1).broadcast_to([P, D])).then_inc(loaded, 16)
            eng.wait_ge(loaded, 192)

        @block.vector
        def _(eng):
            v = Chain(eng, done)
            v.did(eng.memset(one[:, :], 1.0))
            eng.wait_ge(loaded, 192)
            v.did(eng.tensor_scalar(heat[:, :], heat[:, :], 0.1, 5.0, ALU.max, ALU.min))
            v.settled()
            v.did(eng.reciprocal(cool[:, :], heat[:, :]))
            v.settled()
            eng.wait_ge(multiplied, 1)
            for k in range(KH):
                v.did(eng.tensor_tensor(f.wlogit[:, k, :].rearrange("p (h g) -> p h g", h=SH),
                                        joined[k][:, :].rearrange("p (h g) -> p h g", h=SH),
                                        cool[:, :].unsqueeze(2).broadcast_to([P, SH, SG]), ALU.mult))
            v.did(eng.tensor_tensor(f.blogit[:, :].rearrange("p (h g) -> p h g", h=SH),
                                    bias[0:1, :].rearrange("p (h g) -> p h g", h=SH),
                                    cool[0:1, :].unsqueeze(2).broadcast_to([1, SH, SG]), ALU.mult))
            v.settled()

        @block.tensor
        def _(eng):
            eng.wait_ge(loaded, 192)
            eng.wait_ge(done, 1)
            for h in range(SH):
                for k in range(KH):
                    eng.matmul(joined[k][:, h * SG:(h + 1) * SG], wxt[:, h, k * P:(k + 1) * P], wslice[:, :],
                               start=True, stop=True)
                eng.matmul(bias[0:1, h * SG:(h + 1) * SG], bx[:, h:h + 1], wslice[:, :], start=True, stop=False)
                mm = eng.matmul(bias[0:1, h * SG:(h + 1) * SG], one[:, :], bslice[:, :], start=False, stop=True)
            mm.then_inc(multiplied, 1)


def slice_tokens(nc, b, f):
    with Phase(nc) as ctx:
        sem = lambda name: ctx.semaphore(name)
        sb = lambda name, shape: ctx.enter_context(nc.sbuf_tensor(name, shape, F32))
        pb = lambda name: ctx.enter_context(nc.psum_tensor(name, [P, BANK], F32))
        xn = [sb(f"k_xn{s}", [P, ACCW]) for s in range(2)]
        xt = [sb(f"k_xt{s}", [P, KH, P]) for s in range(2)]
        top = [sb(f"k_top{s}", [P, SH]) for s in range(2)]
        total = sb("k_total", [P, SH])
        share = sb("k_share", [P, SH])
        weight = [sb(f"k_weight{s}", [P, INNER]) for s in range(2)]
        soft = [sb(f"k_soft{s}", [P, INNER]) for s in range(2)]
        turned = pb("k_turned")
        logits = [pb(f"k_logits{s}") for s in range(2)]
        flipped = pb("k_flipped")
        normed = sem("k_normed")
        ones = sem("k_ones")
        transposed = sem("k_transposed")
        copied = sem("k_copied")
        scored = sem("k_scored")
        topped = sem("k_topped")
        lowered = sem("k_lowered")
        raised = sem("k_raised")
        totalled = sem("k_totalled")
        softened = sem("k_softened")
        flipdone = sem("k_flipdone")
        kept = sem("k_kept")
        summed = sem("k_summed")
        block = ctx.enter_context(nc.Block())
        by_head = lambda t: t.rearrange("p (h g) -> p h g", h=SH)
        spread = lambda t: t.unsqueeze(2).broadcast_to([P, SH, SG])

        @block.vector
        def _(eng):
            for s in range(2):
                eng.memset(xn[s][:, D:ACCW], 1.0).then_inc(ones, 1)

            def norm(w, s):
                wait_if(eng, summed, w - 1)
                eng.tensor_scalar(xn[s][:, 0:D], b.x[:, w, :], b.mean[:, bass.ds(w, 1)], b.rstd[:, bass.ds(w, 1)],
                                  ALU.subtract, ALU.mult).then_inc(normed, 1)

            def lower(w, s):
                eng.wait_ge(scored, w + 1)
                eng.tensor_reduce(top[s][:, :], by_head(logits[s][:, :]), AX_X, ALU.max).then_inc(topped, 1)
                eng.wait_ge(topped, w + 1)
                eng.tensor_tensor(by_head(weight[s][:, :]), by_head(logits[s][:, :]), spread(top[s][:, :]),
                                  ALU.subtract).then_inc(lowered, 1)

            def soften(w, s):
                eng.wait_ge(raised, w + 1)
                eng.tensor_reduce(total[:, :], by_head(weight[s][:, :]), AX_X, ALU.add).then_inc(totalled, 1)
                eng.wait_ge(totalled, 2 * w + 1)
                eng.reciprocal(share[:, :], total[:, :]).then_inc(totalled, 1)
                eng.wait_ge(totalled, 2 * w + 2)
                wait_if(eng, summed, w - 1)
                eng.tensor_tensor(by_head(soft[s][:, :]), by_head(weight[s][:, :]), spread(share[:, :]),
                                  ALU.mult).then_inc(softened, 1)

            def body(w, s):
                if not (isinstance(w, int) and w == NW - 1):
                    norm(w + 1, 1 - s)
                soften(w, s)
                if not (isinstance(w, int) and w == NW - 1):
                    lower(w + 1, 1 - s)
            norm(0, 0)
            lower(0, 0)
            each_window(eng, body)
            eng.wait_ge(ones, 2)
            eng.wait_ge(softened, NW)

        @block.scalar
        def _(eng):
            def copy(w, s):
                eng.wait_ge(transposed, w + 1)
                wait_if(eng, scored, w - 1)
                eng.activation(xt[s][:, :, :].rearrange("p k n -> p (k n)"), turned[:, s * D:(s + 1) * D],
                               ACT.Copy).then_inc(copied, 1)

            def grow(w, s):
                eng.wait_ge(lowered, w + 1)
                eng.activation(weight[s][:, :], weight[s][:, :], ACT.Exp).then_inc(raised, 1)

            def keep(w):
                eng.wait_ge(flipdone, w + 1)
                eng.activation(f.swt[:, :, bass.ds(w * P, P)], flipped[:, :].rearrange("p (q n) -> p q n", q=SB),
                               ACT.Copy).then_inc(kept, 1)

            def body(w, s):
                if not (isinstance(w, int) and w == NW - 1):
                    copy(w + 1, 1 - s)
                keep(w)
                if not (isinstance(w, int) and w == NW - 1):
                    grow(w + 1, 1 - s)
            copy(0, 0)
            grow(0, 0)
            each_window(eng, body)
            eng.wait_ge(kept, NW)

        @block.tensor
        def _(eng):
            eng.wait_ge(ones, 2)

            def score(w, s):
                eng.wait_ge(normed, w + 1)
                wait_if(eng, copied, w - 1)
                eng.transpose(turned[:, s * D:s * D + P], xn[s][:, 0:P], b.ident[:, :])
                eng.transpose(turned[:, s * D + P:(s + 1) * D], xn[s][:, P:D], b.ident[:, :]).then_inc(transposed, 1)
                eng.wait_ge(copied, w + 1)
                wait_if(eng, lowered, w - 1)
                for k in range(KH):
                    eng.matmul(logits[s][:, :], xt[s][:, k, :], f.wlogit[:, k, :], start=(k == 0), stop=False)
                eng.matmul(logits[s][:, :], b.ones[0:1, :], f.blogit[:, :], start=False, stop=True).then_inc(scored, 1)

            def tokens(w, s, nodes=P):
                eng.wait_ge(softened, w + 1)
                wait_if(eng, kept, w)
                for q in range(SB):
                    mm = eng.transpose(flipped[:, q * P:(q + 1) * P], soft[s][:, q * P:(q + 1) * P], b.ident[:, :])
                mm.then_inc(flipdone, 1)
                first = isinstance(w, int) and w == 0
                last = isinstance(w, int) and w == NW - 1
                for q in range(SB):
                    mm = eng.matmul(f.tokens[q][:, 0:ACCW], soft[s][0:nodes, q * P:(q + 1) * P], xn[s][0:nodes, :],
                                    start=first, stop=last, skip_group_check=True)
                mm.then_inc(summed, 1)

            def body(w, s):
                if isinstance(w, int) and w == NW - 1:
                    tokens(w, s, LAST)
                else:
                    score(w + 1, 1 - s)
                    tokens(w, s)
            score(0, 0)
            each_window(eng, body)


def slice_attention(nc, b, f):
    with Phase(nc) as ctx:
        sem = lambda name: ctx.semaphore(name)
        sb = lambda name, shape: ctx.enter_context(nc.sbuf_tensor(name, shape, F32))
        pb = lambda name: ctx.enter_context(nc.psum_tensor(name, [P, BANK], F32))
        share = sb("j_share", [P, SB])
        mean = sb("j_mean", [P, SB, ACCW])
        meant = sb("j_meant", [P, KH, INNER])
        norm = sb("j_norm", [1, INNER])
        token = sb("j_token", [SD, INNER])
        qt = sb("j_qt", [SD, INNER])
        kt = sb("j_kt", [SD, INNER])
        val = sb("j_val", [SG, INNER])
        top = sb("j_top", [SG, SH])
        att = sb("j_att", [SG, INNER])
        attt = sb("j_attt", [SG, INNER])
        slot = sb("j_slot", [SD, INNER])
        bank = [pb(f"j_bank{s}") for s in range(4)]
        pe = sem("j_multiplied")
        ve = sem("j_stepped")
        ac = sem("j_raised")
        biased = sem("j_biased")
        block = ctx.enter_context(nc.Block())
        by_head = lambda t: t.rearrange("p (h g) -> p h g", h=SH)
        spread = lambda t: t.unsqueeze(2).broadcast_to([SG, SH, SG])
        head = lambda t, h: t[0:SD, h * SG:(h + 1) * SG]

        @block.gpsimd
        def _(eng):
            eng.tensor_tensor(b.x[:, :, :], b.x[:, :, :], f.bout[:, :].unsqueeze(1).broadcast_to([P, NW, D]),
                              ALU.add).then_inc(biased, 1)
            eng.wait_ge(biased, 1)

        @block.vector
        def _(eng):
            v = Chain(eng, ve)

            def step(instruction):
                v.did(instruction)
                v.settled()

            for q in range(SB):
                v.did(eng.tensor_scalar(share[:, q:q + 1], f.tokens[q][:, D:ACCW], 1e-5, None, ALU.add))
            v.settled()
            step(eng.reciprocal(share[:, :], share[:, :]))
            for q in range(SB):
                v.did(eng.tensor_scalar(mean[:, q, :], f.tokens[q][:, 0:ACCW], share[:, q:q + 1], None, ALU.mult))
            assert v.n == f.steps[0]
            eng.wait_ge(pe, 1)
            for k in range(KH):
                v.did(eng.tensor_copy(meant[:, k, :], bank[k][:, :]))
            v.did(eng.tensor_copy(norm[:, :], bank[2][0:1, :]))
            assert v.n == f.steps[1]
            eng.wait_ge(pe, 2)
            v.did(eng.tensor_copy(token[:, :], bank[3][0:SD, :]))
            assert v.n == f.steps[2]
            eng.wait_ge(pe, 3)
            for out, n in ((qt, 0), (kt, 1), (val, 2)):
                v.did(eng.tensor_copy(out[:, :], bank[n][0:SD, :]))
            assert v.n == f.steps[3]
            eng.wait_ge(pe, 4)
            step(eng.tensor_reduce(top[:, :], by_head(bank[3][0:SG, :]), AX_X, ALU.max))
            step(eng.tensor_tensor(by_head(att[:, :]), by_head(bank[3][0:SG, :]), spread(top[:, :]), ALU.subtract))
            assert v.n == f.steps[4]
            eng.wait_ge(ac, 1)
            step(eng.tensor_reduce(top[:, :], by_head(att[:, :]), AX_X, ALU.add))
            step(eng.reciprocal(top[:, :], top[:, :]))
            step(eng.tensor_tensor(by_head(att[:, :]), by_head(att[:, :]), spread(top[:, :]), ALU.mult))
            assert v.n == f.steps[5]
            eng.wait_ge(pe, 5)
            v.did(eng.tensor_copy(attt[:, :], bank[0][0:SG, :]))
            assert v.n == f.steps[6]
            eng.wait_ge(pe, 6)
            v.did(eng.tensor_copy(slot[:, :], bank[1][0:SD, :]))
            assert v.n == f.steps[7]
            eng.wait_ge(pe, 7)
            for q in range(SB):
                v.did(eng.tensor_copy(f.outp[:, q, :], bank[2 + q // 2][:, (q % 2) * D:(q % 2 + 1) * D]))
            v.settled()

        @block.scalar
        def _(eng):
            eng.wait_ge(ve, f.steps[4])
            eng.activation(att[:, :], att[:, :], ACT.Exp, scale=float(SD) ** -0.5).then_inc(ac, 1)

        @block.tensor
        def _(eng):
            eng.wait_ge(ve, f.steps[0])
            for q in range(SB):
                for k in range(KH):
                    eng.transpose(bank[k][:, q * P:(q + 1) * P], mean[:, q, k * P:(k + 1) * P], b.ident[:, :])
                mm = eng.transpose(bank[2][0:1, q * P:(q + 1) * P], mean[:, q, D:ACCW], b.ident[:, :])
            mm.then_inc(pe, 1)
            eng.wait_ge(ve, f.steps[1])
            for h in range(SH):
                for k in range(KH):
                    eng.matmul(head(bank[3], h), f.wfx[:, k, h * SD:(h + 1) * SD], meant[:, k, h * SG:(h + 1) * SG],
                               start=(k == 0), stop=False)
                mm = eng.matmul(head(bank[3], h), f.bfx[:, h * SD:(h + 1) * SD], norm[:, h * SG:(h + 1) * SG],
                                start=False, stop=True)
            mm.then_inc(pe, 1)
            eng.wait_ge(ve, f.steps[2])
            for n in range(2):
                eng.matmul(bank[n][0:SD, :], f.wqkv[:, n, :], token[:, :], start=True, stop=True)
            for h in range(SH):
                mm = eng.matmul(head(bank[2], h), head(token, h), f.wqkv[:, 2, :], start=True, stop=True)
            mm.then_inc(pe, 1)
            eng.wait_ge(ve, f.steps[3])
            for h in range(SH):
                mm = eng.matmul(head(bank[3], h), head(qt, h), head(kt, h), start=True, stop=True)
            mm.then_inc(pe, 1)
            eng.wait_ge(ve, f.steps[5])
            for h in range(SH):
                mm = eng.transpose(head(bank[0], h), head(att, h), b.ident[0:SG, 0:SG])
            mm.then_inc(pe, 1)
            eng.wait_ge(ve, f.steps[6])
            for h in range(SH):
                mm = eng.matmul(head(bank[1], h), head(val, h), head(attt, h), start=True, stop=True)
            mm.then_inc(pe, 1)
            eng.wait_ge(ve, f.steps[7])
            for h in range(SH):
                q, side = h // 2, h % 2
                mm = eng.matmul(bank[2 + q // 2][side * SG:(side + 1) * SG, (q % 2) * D:(q % 2 + 1) * D],
                                head(slot, h), f.wout[:, h, :], start=True, stop=True)
            mm.then_inc(pe, 1)


def slice_output(nc, b, m, f):
    with Phase(nc) as ctx:
        sem = lambda name: ctx.semaphore(name)
        weight = [ctx.enter_context(nc.sbuf_tensor(f"o_weight{s}", [P, SB, P], F32)) for s in range(2)]
        product = [ctx.enter_context(nc.psum_tensor(f"o_product{s}", [P, BANK], F32)) for s in range(2)]
        copied = sem("o_copied")
        multiplied = sem("o_multiplied")
        added = sem("o_added")
        stored = sem("o_stored")
        block = ctx.enter_context(nc.Block())

        @block.scalar
        def _(eng):
            def body(w, s):
                wait_if(eng, multiplied, w - 1)
                eng.activation(weight[s][:, :, :], f.swt[:, :, bass.ds(w * P, P)], ACT.Copy).then_inc(copied, 1)
            each_window(eng, body)

        @block.tensor
        def _(eng):
            def body(w, s):
                eng.wait_ge(copied, w + 1)
                wait_if(eng, added, w - 1)
                for q in range(SB):
                    mm = eng.matmul(product[s][:, 0:D], weight[s][:, q, :], f.outp[:, q, :],
                                    start=(q == 0), stop=(q == SB - 1))
                mm.then_inc(multiplied, 1)
            each_window(eng, body)

        @block.vector
        def _(eng):
            def body(w, s):
                eng.wait_ge(multiplied, w + 1)
                eng.tensor_tensor(b.x[:, w, :], b.x[:, w, :], product[s][:, 0:D], ALU.add).then_inc(added, 1)
            each_window(eng, body)

        @block.sync
        def _(eng):
            def body(w, s):
                eng.wait_ge(added, w + 1)
                if isinstance(w, int) and w == NW - 1:
                    eng.dma_start(m["out"][w * P:N, :], b.x[0:LAST, w, :]).then_inc(stored, 16)
                else:
                    eng.dma_start(m["out"][bass.ds(w * P, P), :], b.x[:, w, :]).then_inc(stored, 16)
            each_window(eng, body)
            eng.wait_ge(stored, 16 * NW)


def slice_phase(nc, b, m):
    with ExitStack() as ctx:
        sb = lambda name, shape: ctx.enter_context(nc.sbuf_tensor(name, shape, F32))
        f = Named()
        f.steps = [9, 12, 13, 16, 18, 21, 22, 23]
        f.wlogit = sb("wlogit", [P, KH, INNER])
        f.blogit = sb("blogit", [1, INNER])
        f.wfx = sb("wfx", [P, KH, INNER])
        f.bfx = sb("bfx", [1, INNER])
        f.wout = sb("wout", [SD, SH, D])
        f.wqkv = sb("wqkv", [SD, 3, SD])
        f.bout = sb("bout", [P, D])
        f.outp = sb("outp", [P, SB, D])
        f.swt = sb("swt", [P, SB, NP])
        slice_weights(nc, m, f)
        with ExitStack() as inner:
            f.tokens = [inner.enter_context(nc.psum_tensor(f"tokens{q}", [P, BANK], F32)) for q in range(SB)]
            slice_tokens(nc, b, f)
            slice_attention(nc, b, f)
        slice_output(nc, b, m, f)



def build(nc, m):
    table1 = nc.dram_tensor("table1", [NP, RELS * D], F32).ap()
    m["table1"] = table1
    m["table2"] = nc.dram_tensor("table2", [NP, D], F32).ap()
    m["scr_base"] = nc.dram_tensor("scr_base", [NG], I32).ap()
    m["scr_span"] = nc.dram_tensor("scr_span", [NG], I32).ap()
    with ExitStack() as ctx:
        sb = lambda name, shape, dt=F32: ctx.enter_context(nc.sbuf_tensor(name, shape, dt))
        b = Named()
        b.x = sb("features", [P, NW, D])
        b.ident = sb("ident", [P, P])
        b.ones = sb("ones", [P, P])
        b.ramp = sb("ramp", [P, 2 * P])
        b.wstart = sb("wstart", [P, NW])
        b.mean = sb("mean", [P, NW])
        b.rstd = sb("rstd", [P, NW])
        with ExitStack() as inner:
            ib = lambda name, shape, dt=F32: inner.enter_context(nc.sbuf_tensor(name, shape, dt))
            big = ib("big", [P, NW * ACCW])
            b.acc = big[:, :].rearrange("p (w c) -> p w c", c=ACCW)
            b.xt = big[:, 0:KH * NP].rearrange("p (k n) -> p k n", k=KH)
            b.degree = ib("degree", [P, NW])
            b.esrc = ib("esrc", [P, NT], I32)
            b.edsti = ib("edsti", [P, NT], I32)
            b.edst = ib("edst", [P, NT])
            b.wbase = ib("wbase", [1, NG], I32)
            b.maxspan = ib("maxspan", [1, 1], I32)
            with ExitStack() as first:
                b.erow = first.enter_context(nc.sbuf_tensor("erow", [P, NT], I32))
                constants(nc, b, m)
                row_statistics(nc, b, "ln1")
                relation_table(nc, b, m)
                relation_rows = table1.rearrange("n (r d) -> (n r) d", d=D)
                edge_sums(nc, b, relation_rows, b.erow, "e1")
                far_edges(nc, b, relation_rows, b.erow, "f1")
            add_relations(nc, b, m)
            row_statistics(nc, b, "ln2")
            attention_phase(nc, b, m)
            row_statistics(nc, b, "ln3")
            sparse_table(nc, b, m)
            edge_sums(nc, b, m["table2"], b.esrc, "e2")
            far_edges(nc, b, m["table2"], b.esrc, "f2")
            add_neighbours(nc, b)
        row_statistics(nc, b, "ln4")
        slice_phase(nc, b, m)



def laid_out(i, np):
    pad = NT * P - E
    columns = lambda a: np.ascontiguousarray(a.reshape(-1, P).T)
    rows = lambda a, fill: np.concatenate([a, np.full(pad, fill, a.dtype)])
    src, kind, dst = rows(i["src"], 0), rows(i["edge_type_8"], 0), rows(i["dst"], NOWHERE)
    edge = i["L0_ffn_edge_index"]
    return {
        "x": np.concatenate([i["x"], np.zeros((NP - N, D), i["x"].dtype)]),
        "src_cols": columns(src), "type_cols": columns(kind), "dst_cols": columns(dst),
        "dst_rows": dst.reshape(GROWS, NG // GROWS, GROUP * P),
        "gsrc_cols": columns(edge[0]), "gdst_cols": columns(edge[1]),
        "weight": i["L0_gnn_weight"], "h_bias": i["L0_gnn_h_bias"], "loop_weight": i["L0_gnn_loop_weight"],
        "W_gat": i["L0_ffn_W_gat"], "att_src": i["L0_ffn_att_src"], "att_dst": i["L0_ffn_att_dst"],
        "b_gat": i["L0_ffn_b_gat"], "ln_gamma": i["L0_ffn_ln_gamma"], "ln_beta": i["L0_ffn_ln_beta"],
        "W1": i["L0_ffn_W1"], "b1": i["L0_ffn_b1"], "W2": i["L0_ffn_W2"], "b2": i["L0_ffn_b2"],
        "W_self": i["L1_gnn_W_self"], "W_neigh": i["L1_gnn_W_neigh"],
        "W_fx": i["L1_ffn_W_fx"], "b_fx": i["L1_ffn_b_fx"],
        "W_xT": i["L1_ffn_W_x"].T, "b_x_cols": i["L1_ffn_b_x"].reshape(SH, SD).T,
        "W_slice": i["L1_ffn_W_slice"], "b_slice": i["L1_ffn_b_slice"],
        "W_q": i["L1_ffn_W_q"], "W_k": i["L1_ffn_W_k"], "W_v": i["L1_ffn_W_v"],
        "W_out": i["L1_ffn_W_out"], "b_out": i["L1_ffn_b_out"],
        "temperature": i["L1_ffn_temperature"].reshape(SH),
    }


def kernel(**inputs):
    import numpy as np
    import concourse.bacc as bacc
    from concourse.bass_utils import run_bass_kernel_spmd

    nc = bacc.Bacc("TRN2", target_bir_lowering=False, num_devices=1)
    arrays = laid_out({name: np.asarray(a) for name, a in inputs.items()}, np)
    arrays = {f"in_{name}": np.ascontiguousarray(a) for name, a in arrays.items()}
    m = {name[3:]: nc.dram_tensor(name, a.shape, mybir.dt.from_np(a.dtype), kind="ExternalInput").ap()
         for name, a in arrays.items()}
    m["out"] = nc.dram_tensor("out", [N, D], F32, kind="ExternalOutput").ap()
    build(nc, m)
    return run_bass_kernel_spmd(nc, [arrays], core_ids=[0]).results[0]["out"]
```
